# Optimizing a Trainium2 kernel written in Bass

```python
import numpy as np
import jax
import jax.numpy as jnp

def _softmax(x, axis=-1):
    return jax.nn.softmax(x, axis=axis)

def _gelu(x):
    return jax.nn.gelu(x, approximate=True)

def _silu(x):
    return jax.nn.silu(x)

def _sigmoid(x):
    return jax.nn.sigmoid(x)

def _layernorm(x, axis=-1, eps=1e-05):
    m = jnp.mean(x, axis=axis, keepdims=True)
    v = jnp.var(x, axis=axis, keepdims=True)
    return (x - m) / jnp.sqrt(v + eps)

def _scatter_add(tgt, idx, src, axis=0):
    return tgt.at[idx].add(src)

def _segment_sum(src, seg, n):
    return jax.ops.segment_sum(src, seg, n)
kernel_name = 'mk_vit_tower_d2_tok_img256_r4_4433f8'

def setup_inputs(seed: int=0):
    np.random.seed(seed)
    _w = jnp.asarray

    def _rec_inputs():
        import jax
        import jax.numpy as jnp
        _rk = jax.random.key(seed)
        x = -0.000596345 + 1.00056 * jax.random.normal(jax.random.fold_in(_rk, 1), (64, 64, 64, 3), jnp.float32)
        return x
    x = _rec_inputs()

    def _L0_tok_setup():
        import jax, jax.numpy as jnp
        import numpy as np
        M1 = 20
        M2 = 20

        def _spectral_conv(x, w):
            B, Cin, H, W = x.shape
            x_ft = jnp.fft.rfft2(x, norm='ortho')
            out = jnp.einsum('bixy,ioxy->boxy', x_ft[:, :, :M1, :M2], w.astype(x_ft.dtype))
            out_ft = jnp.zeros((B, w.shape[1], H, W // 2 + 1), dtype=x_ft.dtype)
            out_ft = out_ft.at[:, :, :M1, :M2].set(out)
            return jnp.fft.irfft2(out_ft, s=(H, W), norm='ortho')

        def _gelu(x):
            return jax.nn.gelu(x, approximate=False)
        key = jax.random.key(seed)
        ks = jax.random.split(key, 16)
        B, H, W, width = (16, 64, 64, 32)
        scale = 1.0 / (width * width)
        d = {}
        d['coords'] = jax.random.normal(ks[0], (B, H, W, 3), dtype=jnp.float32)
        d['fc0_w'] = jax.random.normal(ks[1], (3, width), dtype=jnp.float32) * 0.1
        d['fc0_b'] = jnp.zeros((width,), dtype=jnp.float32)
        for i in range(4):
            d[f'sw{i}'] = scale * jax.random.normal(ks[2 + i], (width, width, M1, M2), dtype=jnp.float32)
            d[f'cw{i}'] = jax.random.normal(ks[6 + i], (width, width), dtype=jnp.float32) * 0.1
            d[f'cb{i}'] = jnp.zeros((width,), dtype=jnp.float32)
        d['fc1_w'] = jax.random.normal(ks[10], (width, 64), dtype=jnp.float32) * 0.1
        d['fc1_b'] = jnp.zeros((64,), dtype=jnp.float32)
        d['fc2_w'] = jax.random.normal(ks[11], (64, 1), dtype=jnp.float32) * 0.1
        d['fc2_b'] = jnp.zeros((1,), dtype=jnp.float32)
        return d
    _L0_tok_all = _L0_tok_setup()
    _L0_tok_in = {k: v for k, v in _L0_tok_all.items() if k in ('fc0_w', 'fc0_b', 'sw0', 'cw0', 'cb0', 'sw1', 'cw1', 'cb1', 'sw2', 'cw2', 'cb2', 'sw3', 'cw3', 'cb3', 'fc1_w', 'fc1_b', 'fc2_w', 'fc2_b')}
    del _L0_tok_all

    def _L0_attn_setup():
        import jax, jax.numpy as jnp
        import numpy as np
        NHEAD = 8
        ATT_EPS = 1e-06
        LN_EPS = 1e-05

        def _layernorm(x, g, b):
            mu = jnp.mean(x, axis=-1, keepdims=True)
            var = jnp.mean(jnp.square(x - mu), axis=-1, keepdims=True)
            return (x - mu) * jax.lax.rsqrt(var + LN_EPS) * g + b
        key = jax.random.key(seed)
        ks = jax.random.split(key, 7)
        N, L, C = (4, 4096, 64)
        s = 1.0 / np.sqrt(C)
        return {'x': jax.random.normal(ks[0], (N, L, C), jnp.float32), 'Wq': jax.random.normal(ks[1], (C, C), jnp.float32) * s, 'Wk': jax.random.normal(ks[2], (C, C), jnp.float32) * s, 'Wv': jax.random.normal(ks[3], (C, C), jnp.float32) * s, 'Wm': jax.random.normal(ks[4], (C, C), jnp.float32) * s, 'W1': jax.random.normal(ks[5], (2 * C, 2 * C), jnp.float32) * (1.0 / np.sqrt(2 * C)), 'W2': jax.random.normal(ks[6], (2 * C, C), jnp.float32) * (1.0 / np.sqrt(2 * C)), 'g1': jnp.ones((C,), jnp.float32), 'b1': jnp.zeros((C,), jnp.float32), 'g2': jnp.ones((C,), jnp.float32), 'b2': jnp.zeros((C,), jnp.float32)}
    _L0_attn_all = _L0_attn_setup()
    _L0_attn_in = {k: v for k, v in _L0_attn_all.items() if k in ('Wq', 'Wk', 'Wv', 'Wm', 'W1', 'W2', 'g1', 'b1', 'g2', 'b2')}
    del _L0_attn_all

    def _L0_ffn_setup():
        import jax, jax.numpy as jnp
        import numpy as np
        B, K, D = (128, 16, 64)
        E = 32
        H = int(D * 0.25)
        key = jax.random.key(seed)
        ks = jax.random.split(key, 7)
        d_rs = D ** (-0.5)
        h_rs = H ** (-0.5)
        x = jax.random.normal(ks[0], (B, K, D), dtype=jnp.float32)
        router_w = jax.random.uniform(ks[1], (E, D), jnp.float32, -d_rs, d_rs)
        router_b = jax.random.uniform(ks[2], (E,), jnp.float32, -d_rs, d_rs)
        W1 = jax.random.uniform(ks[3], (E, D, H), jnp.float32, -h_rs, h_rs)
        b1 = jax.random.uniform(ks[4], (E, H), jnp.float32, -h_rs, h_rs)
        W2 = jax.random.uniform(ks[5], (E, H, D), jnp.float32, -d_rs, d_rs)
        b2 = jax.random.uniform(ks[6], (E, D), jnp.float32, -d_rs, d_rs)
        return {'x': x, 'router_w': router_w, 'router_b': router_b, 'W1': W1, 'b1': b1, 'W2': W2, 'b2': b2}
    _L0_ffn_all = _L0_ffn_setup()
    _L0_ffn_in = {k: v for k, v in _L0_ffn_all.items() if k in ('router_w', 'router_b', 'W1', 'b1', 'W2', 'b2')}
    del _L0_ffn_all

    def _L1_attn_setup():
        import jax, jax.numpy as jnp
        import numpy as np
        B, S, C = (8, 256, 64)
        H, KD = (8, 64)
        HEAD_DIM = KD // H
        key = jax.random.key(seed)
        ks = jax.random.split(key, 5)
        sc = 0.02
        return {'x': jax.random.normal(ks[0], (B, S, C), dtype=jnp.float32), 'Wq': jax.random.normal(ks[1], (H * KD, C), dtype=jnp.float32) * sc, 'Wk': jax.random.normal(ks[2], (KD, C), dtype=jnp.float32) * sc, 'Wv': jax.random.normal(ks[3], (KD, C), dtype=jnp.float32) * sc, 'Wo': jax.random.normal(ks[4], (C, H * KD), dtype=jnp.float32) * sc}
    _L1_attn_all = _L1_attn_setup()
    _L1_attn_in = {k: v for k, v in _L1_attn_all.items() if k in ('Wq', 'Wk', 'Wv', 'Wo')}
    del _L1_attn_all

    def _L1_ffn_setup():
        import jax, jax.numpy as jnp
        import numpy as np
        C = 64
        HID = 256
        E = 8
        TEMP = 1.0
        key = jax.random.key(seed)
        ks = jax.random.split(key, 7)
        x = jax.random.normal(ks[0], (8, 4096, C), dtype=jnp.float32)
        W1 = jax.random.normal(ks[1], (C, HID), dtype=jnp.float32) * 0.02
        b1 = jnp.zeros((HID,), dtype=jnp.float32)
        Wg = jax.random.normal(ks[2], (HID, E), dtype=jnp.float32) * 0.02
        bg = jnp.zeros((E,), dtype=jnp.float32)
        Wd = jax.random.normal(ks[3], (E, HID, C), dtype=jnp.float32) * 0.02
        bd = jnp.zeros((E, C), dtype=jnp.float32)
        return {'x': x, 'W1': W1, 'b1': b1, 'Wg': Wg, 'bg': bg, 'Wd': Wd, 'bd': bd}
    _L1_ffn_all = _L1_ffn_setup()
    _L1_ffn_in = {k: v for k, v in _L1_ffn_all.items() if k in ('W1', 'b1', 'Wg', 'bg', 'Wd', 'bd')}
    del _L1_ffn_all
    return {'x': x, 'L0_tok_fc0_w': _L0_tok_in['fc0_w'], 'L0_tok_fc0_b': _L0_tok_in['fc0_b'], 'L0_tok_sw0': _L0_tok_in['sw0'], 'L0_tok_cw0': _L0_tok_in['cw0'], 'L0_tok_cb0': _L0_tok_in['cb0'], 'L0_tok_sw1': _L0_tok_in['sw1'], 'L0_tok_cw1': _L0_tok_in['cw1'], 'L0_tok_cb1': _L0_tok_in['cb1'], 'L0_tok_sw2': _L0_tok_in['sw2'], 'L0_tok_cw2': _L0_tok_in['cw2'], 'L0_tok_cb2': _L0_tok_in['cb2'], 'L0_tok_sw3': _L0_tok_in['sw3'], 'L0_tok_cw3': _L0_tok_in['cw3'], 'L0_tok_cb3': _L0_tok_in['cb3'], 'L0_tok_fc1_w': _L0_tok_in['fc1_w'], 'L0_tok_fc1_b': _L0_tok_in['fc1_b'], 'L0_tok_fc2_w': _L0_tok_in['fc2_w'], 'L0_tok_fc2_b': _L0_tok_in['fc2_b'], 'L0_attn_Wq': _L0_attn_in['Wq'], 'L0_attn_Wk': _L0_attn_in['Wk'], 'L0_attn_Wv': _L0_attn_in['Wv'], 'L0_attn_Wm': _L0_attn_in['Wm'], 'L0_attn_W1': _L0_attn_in['W1'], 'L0_attn_W2': _L0_attn_in['W2'], 'L0_attn_g1': _L0_attn_in['g1'], 'L0_attn_b1': _L0_attn_in['b1'], 'L0_attn_g2': _L0_attn_in['g2'], 'L0_attn_b2': _L0_attn_in['b2'], 'L0_ffn_router_w': _L0_ffn_in['router_w'], 'L0_ffn_router_b': _L0_ffn_in['router_b'], 'L0_ffn_W1': _L0_ffn_in['W1'], 'L0_ffn_b1': _L0_ffn_in['b1'], 'L0_ffn_W2': _L0_ffn_in['W2'], 'L0_ffn_b2': _L0_ffn_in['b2'], 'L1_attn_Wq': _L1_attn_in['Wq'], 'L1_attn_Wk': _L1_attn_in['Wk'], 'L1_attn_Wv': _L1_attn_in['Wv'], 'L1_attn_Wo': _L1_attn_in['Wo'], 'L1_ffn_W1': _L1_ffn_in['W1'], 'L1_ffn_b1': _L1_ffn_in['b1'], 'L1_ffn_Wg': _L1_ffn_in['Wg'], 'L1_ffn_bg': _L1_ffn_in['bg'], 'L1_ffn_Wd': _L1_ffn_in['Wd'], 'L1_ffn_bd': _L1_ffn_in['bd']}

def reference(x, L0_tok_fc0_w, L0_tok_fc0_b, L0_tok_sw0, L0_tok_cw0, L0_tok_cb0, L0_tok_sw1, L0_tok_cw1, L0_tok_cb1, L0_tok_sw2, L0_tok_cw2, L0_tok_cb2, L0_tok_sw3, L0_tok_cw3, L0_tok_cb3, L0_tok_fc1_w, L0_tok_fc1_b, L0_tok_fc2_w, L0_tok_fc2_b, L0_attn_Wq, L0_attn_Wk, L0_attn_Wv, L0_attn_Wm, L0_attn_W1, L0_attn_W2, L0_attn_g1, L0_attn_b1, L0_attn_g2, L0_attn_b2, L0_ffn_router_w, L0_ffn_router_b, L0_ffn_W1, L0_ffn_b1, L0_ffn_W2, L0_ffn_b2, L1_attn_Wq, L1_attn_Wk, L1_attn_Wv, L1_attn_Wo, L1_ffn_W1, L1_ffn_b1, L1_ffn_Wg, L1_ffn_bg, L1_ffn_Wd, L1_ffn_bd):
    import jax
    import jax.numpy as jnp

    def _L0_tok_ref(coords, fc0_w, fc0_b, sw0, cw0, cb0, sw1, cw1, cb1, sw2, cw2, cb2, sw3, cw3, cb3, fc1_w, fc1_b, fc2_w, fc2_b):
        import jax, jax.numpy as jnp
        import numpy as np
        M1 = 20
        M2 = 20

        def _spectral_conv(x, w):
            B, Cin, H, W = x.shape
            x_ft = jnp.fft.rfft2(x, norm='ortho')
            out = jnp.einsum('bixy,ioxy->boxy', x_ft[:, :, :M1, :M2], w.astype(x_ft.dtype))
            out_ft = jnp.zeros((B, w.shape[1], H, W // 2 + 1), dtype=x_ft.dtype)
            out_ft = out_ft.at[:, :, :M1, :M2].set(out)
            return jnp.fft.irfft2(out_ft, s=(H, W), norm='ortho')

        def _gelu(x):
            return jax.nn.gelu(x, approximate=False)
        x = coords @ fc0_w + fc0_b
        x = jnp.transpose(x, (0, 3, 1, 2))
        for sw, cw, cb in ((sw0, cw0, cb0), (sw1, cw1, cb1), (sw2, cw2, cb2), (sw3, cw3, cb3)):
            x1 = _spectral_conv(x, sw)
            x2 = jnp.einsum('bchw,oc->bohw', x, cw) + cb[None, :, None, None]
            x = _gelu(x1 + x2)
        x = jnp.transpose(x, (0, 2, 3, 1))
        x = _gelu(x @ fc1_w + fc1_b)
        return (x @ fc2_w + fc2_b)[..., 0]

    def _L0_attn_ref(x, Wq, Wk, Wv, Wm, W1, W2, g1, b1, g2, b2):
        import jax, jax.numpy as jnp
        import numpy as np
        NHEAD = 8
        ATT_EPS = 1e-06
        LN_EPS = 1e-05

        def _layernorm(x, g, b):
            mu = jnp.mean(x, axis=-1, keepdims=True)
            var = jnp.mean(jnp.square(x - mu), axis=-1, keepdims=True)
            return (x - mu) * jax.lax.rsqrt(var + LN_EPS) * g + b
        N, L, C = x.shape
        H = NHEAD
        D = C // H
        q = (x @ Wq).reshape(N, L, H, D)
        k = (x @ Wk).reshape(N, L, H, D)
        v = (x @ Wv).reshape(N, L, H, D)
        Q = jax.nn.elu(q) + 1.0
        K = jax.nn.elu(k) + 1.0
        v = v / L
        KV = jnp.einsum('nshd,nshv->nhdv', K, v)
        Z = 1.0 / (jnp.einsum('nlhd,nhd->nlh', Q, K.sum(axis=1)) + ATT_EPS)
        msg = jnp.einsum('nlhd,nhdv,nlh->nlhv', Q, KV, Z) * L
        msg = msg.reshape(N, L, C) @ Wm
        msg = _layernorm(msg, g1, b1)
        h = jnp.concatenate([x, msg], axis=-1) @ W1
        h = jax.nn.relu(h) @ W2
        msg = _layernorm(h, g2, b2)
        return x + msg

    def _L0_ffn_ref(x, router_w, router_b, W1, b1, W2, b2):
        import jax, jax.numpy as jnp
        import numpy as np
        B, K, D = (128, 16, 64)
        E = 32
        H = int(D * 0.25)
        xf = x.reshape(-1, D)
        logits = xf @ router_w.T + router_b
        idx = jnp.argmax(logits, axis=-1)
        w1t = jnp.take(W1, idx, axis=0)
        h = jnp.einsum('nd,ndh->nh', xf, w1t) + jnp.take(b1, idx, axis=0)
        h = jax.nn.relu(h)
        w2t = jnp.take(W2, idx, axis=0)
        out = jnp.einsum('nh,nhd->nd', h, w2t) + jnp.take(b2, idx, axis=0)
        out = jax.nn.relu(out)
        return out.reshape(x.shape)

    def _L1_attn_ref(x, Wq, Wk, Wv, Wo):
        import jax, jax.numpy as jnp
        import numpy as np
        B, S, C = (8, 256, 64)
        H, KD = (8, 64)
        HEAD_DIM = KD // H
        b, s, c = x.shape
        q = jnp.einsum('bsc,oc->bso', x, Wq).reshape(b, s, H, KD).transpose(0, 2, 1, 3)
        k = jnp.einsum('bsc,oc->bos', x, Wk)
        v_conv = jnp.einsum('bsc,oc->bos', x, Wv)
        v = v_conv.reshape(b, s, KD)
        scale = 1.0 / np.sqrt(HEAD_DIM).astype(np.float32)
        scores = jnp.einsum('bhsd,bdt->bhst', q, k) * scale
        attn = jax.nn.softmax(scores, axis=-1)
        ctx = jnp.einsum('bhst,btd->bhsd', attn, v)
        ctx = ctx.transpose(0, 2, 1, 3).reshape(b, H * KD, s)
        out = jnp.einsum('bcp,oc->bop', ctx, Wo)
        return out.transpose(0, 2, 1)

    def _L1_ffn_ref(x, W1, b1, Wg, bg, Wd, bd):
        import jax, jax.numpy as jnp
        import numpy as np
        C = 64
        HID = 256
        E = 8
        TEMP = 1.0
        orig_shape = x.shape
        xf = x.reshape(-1, orig_shape[-1])
        H = jax.nn.gelu(xf @ W1 + b1, approximate=False)
        probs = jax.nn.softmax((H @ Wg + bg) / TEMP, axis=-1)
        assign = jnp.argmax(probs, axis=-1)
        out = jnp.zeros_like(xf)
        for e in range(Wd.shape[0]):
            y = H @ Wd[e] + bd[e]
            sel = (assign == e)[:, None]
            out = out + jnp.where(sel, probs[:, e:e + 1] * y, 0.0)
        return out.reshape(orig_shape)
    h = _L0_tok_ref(x, L0_tok_fc0_w, L0_tok_fc0_b, L0_tok_sw0, L0_tok_cw0, L0_tok_cb0, L0_tok_sw1, L0_tok_cw1, L0_tok_cb1, L0_tok_sw2, L0_tok_cw2, L0_tok_cb2, L0_tok_sw3, L0_tok_cw3, L0_tok_cb3, L0_tok_fc1_w, L0_tok_fc1_b, L0_tok_fc2_w, L0_tok_fc2_b)
    h = h + _L0_attn_ref(_layernorm(h, axis=-1), L0_attn_Wq, L0_attn_Wk, L0_attn_Wv, L0_attn_Wm, L0_attn_W1, L0_attn_W2, L0_attn_g1, L0_attn_b1, L0_attn_g2, L0_attn_b2)
    h = h + _L0_ffn_ref(_layernorm(h, axis=-1), L0_ffn_router_w, L0_ffn_router_b, L0_ffn_W1, L0_ffn_b1, L0_ffn_W2, L0_ffn_b2)
    h = h + _L1_attn_ref(_layernorm(h, axis=-1), L1_attn_Wq, L1_attn_Wk, L1_attn_Wv, L1_attn_Wo)
    h = h + _L1_ffn_ref(_layernorm(h, axis=-1), L1_ffn_W1, L1_ffn_b1, L1_ffn_Wg, L1_ffn_bg, L1_ffn_Wd, L1_ffn_bd)
    return h

_drawn_inputs = setup_inputs


def setup_inputs(seed=0):
    import zlib

    import numpy as np

    out = dict(_drawn_inputs(seed))
    spreads = {'L0_tok_fc0_b': (0.0, 0.1),
     'L0_tok_cb0': (0.0, 0.1),
     'L0_tok_cb1': (0.0, 0.1),
     'L0_tok_cb2': (0.0, 0.1),
     'L0_tok_cb3': (0.0, 0.1),
     'L0_tok_fc1_b': (0.0, 0.1),
     'L0_attn_g1': (1.0, 0.2),
     'L0_attn_b1': (0.0, 0.1),
     'L0_attn_g2': (1.0, 0.2),
     'L0_attn_b2': (0.0, 0.1),
     'L1_ffn_b1': (0.0, 0.8),
     'L1_ffn_bg': (0.0, 0.445),
     'L1_ffn_bd': (0.0, 0.558)}
    factors = {'L0_tok_sw3': 2.721,
     'L0_attn_Wq': 7.877,
     'L0_ffn_b1': 2.844,
     'L1_attn_Wq': 8.0,
     'L1_attn_Wk': 8.0,
     'L1_attn_Wv': 6.445,
     'L1_attn_Wo': 5.152,
     'L1_ffn_W1': 4.686,
     'L1_ffn_Wg': 8.0,
     'L1_ffn_Wd': 8.0}
    for name, (base, spread) in spreads.items():
        noise = np.random.default_rng([zlib.crc32(name.encode()), seed]).standard_normal(out[name].shape)
        drawn = base * np.exp(spread * noise) if base else spread * noise
        out[name] = jnp.asarray(drawn.astype(out[name].dtype))
    for name, factor in factors.items():
        out[name] = (out[name] * factor).astype(out[name].dtype)
    return out
```

```python
from contextlib import ExitStack

import numpy as np
import concourse.bass as bass
from concourse import mybir

F32 = mybir.dt.float32
ALU = mybir.AluOpType
ACT = mybir.ActivationFunctionType
AX = mybir.AxisListType

IMAGES, HEIGHT, WIDTH = 64, 64, 64
CH = 32
MODES = 20
LAYERS = 4
HID = 64
J = 4
QUARTERS = 4
QIMG = IMAGES // QUARTERS
GROUPS = QIMG // 4
PIX = HEIGHT * WIDTH
UNITS = 8
KYQ = MODES // 4
KXM = MODES // 2
TURN_KYQ = 3
TURNS = -(-KYQ // TURN_KYQ)
ROW_USES = 6
PACK = 3
PACK_K = PACK * 2 * MODES
PACKS = ((0, 0, 0, 3), (3, 0, 3, 3), (5, PACK * WIDTH, 6, 2))
WIDE = 96
BANKS = 4


def tower_stages():
    for g in range(GROUPS):
        yield 0, "coord_rows", g, 0
    for g in range(GROUPS):
        for p in range(2):
            yield 0, "coord_spec", g, p
    for n in range(2 * GROUPS):
        yield 0, "lift", n, 0
    for layer in range(LAYERS):
        last = layer == LAYERS - 1
        for kyq in range(KYQ):
            yield layer, "mix", kyq, 0
            yield layer, "mix", kyq, 1
        for part in range(TURNS):
            yield layer, "turn", 0, part
        for kyq in range(KYQ):
            yield layer, "cols", 0, kyq
        yield layer, "part", 0, 0
        for g in range(GROUPS):
            for u in range(UNITS):
                if u + 1 < UNITS:
                    yield layer, "part", g, u + 1
                if g + 1 < GROUPS and 1 <= u <= TURNS:
                    yield layer, "turn", g + 1, u - 1
                yield layer, "z", g, u
                if g + 1 < GROUPS and u >= 6:
                    for kyq in ((0, 1, 2), (3, 4))[u - 6]:
                        yield layer, "cols", g + 1, kyq
                if last:
                    if u == 5:
                        yield layer, "fc2", g, 0
                    if u == 1 and g >= 1:
                        yield layer, "fc2", g - 1, 1
                    if u >= 1:
                        yield layer, "fc1", g, u - 1
                    continue
                if g >= 1 and u < 2:
                    yield layer, "pix", g - 1, UNITS - 2 + u
                if g >= 1 and u == 2:
                    for n in range(ROW_USES):
                        yield layer, "rows", g - 1, n
                if u >= 2:
                    yield layer, "pix", g, u - 2
                if g >= 1 and u == 4:
                    yield layer, "spec", g - 1, 0
                    yield layer, "spec", g - 1, 1
            if last:
                yield layer, "fc1", g, UNITS - 1
            if g + 1 < GROUPS:
                yield layer, "part", g + 1, 0
        if last:
            yield layer, "fc2", GROUPS - 1, 1
        else:
            g = GROUPS - 1
            yield layer, "pix", g, UNITS - 2
            yield layer, "pix", g, UNITS - 1
            for n in range(ROW_USES):
                yield layer, "rows", g, n
            yield layer, "spec", g, 0
            yield layer, "spec", g, 1


def in_ring(stage):
    return stage[1] not in ("z", "fc1")


RING_USES = sum(in_ring(s) for s in tower_stages())
Z_UNITS = LAYERS * GROUPS * UNITS
HEAD_UNITS = GROUPS * UNITS
assert RING_USES % BANKS == 0


def ring_counts():
    at, out = 0, {}
    for s in tower_stages():
        at += in_ring(s)
        out[s] = at
    return out


AFTER = ring_counts()


def fourier_tables():
    t64 = 2 * np.pi / 64
    w = np.arange(64)
    rows = np.zeros((2, 64, 2, 2, MODES))
    for p in range(2):
        for h1 in range(2):
            sign = (-1.0) ** (p * h1)
            a = t64 * np.outer(w, np.arange(MODES))
            rows[h1, :, p, 0, :] = sign * np.cos(a)
            rows[h1, :, p, 1, :] = -sign * np.sin(a)
    spec = np.zeros((32, 4, 2, 2, 4, KXM, 2))
    for b in range(4):
        for p in range(2):
            a = t64 * np.outer(np.arange(32), 2 * np.arange(KXM) + p)
            spec[:, b, p, 0, b, :, 0] = np.cos(a) / 64
            spec[:, b, p, 0, b, :, 1] = -np.sin(a) / 64
            spec[:, b, p, 1, b, :, 0] = np.sin(a) / 64
            spec[:, b, p, 1, b, :, 1] = np.cos(a) / 64
    cols = np.zeros((128, TURN_KYQ, 32, 2, 2))
    h = np.arange(32)[:, None] + 32 * np.arange(2)[None, :]
    for p in range(2):
        for m in range(KXM):
            a = t64 * (2 * m + p) * h
            for k in range(TURN_KYQ):
                r = k * 2 * MODES + (p * KXM + m) * 2
                cols[r, k, :, :, 0], cols[r + 1, k, :, :, 0] = np.cos(a), -np.sin(a)
                cols[r, k, :, :, 1], cols[r + 1, k, :, :, 1] = np.sin(a), np.cos(a)
    pix = np.zeros((PACK, 2, MODES, PACK + 2, 64))
    for ky in range(MODES):
        c = (1.0 if ky == 0 else 2.0) / 64
        for row in range(PACK):
            for to in (row, PACK + row - 1)[:1 if row == 0 else 2]:
                pix[row, 0, ky, to] = c * np.cos(t64 * ky * w)
                pix[row, 1, ky, to] = -c * np.sin(t64 * ky * w)
    f = np.float32
    wide = ((0, 0), (0, 0), (0, WIDE - 80))
    return {"rows": np.pad(rows.reshape(128, 1, 80), wide).reshape(128, WIDE).astype(f),
            "spec": np.pad(spec.reshape(128, 4, 80), wide).reshape(128, 4 * WIDE).astype(f),
            "cols": cols.reshape(128, TURN_KYQ * 128).astype(f), "pix": pix.reshape(PACK_K, (PACK + 2) * WIDTH).astype(f)}


def tower(nc, ctx, d, tok):
    def sb(name, shape):
        return ctx.enter_context(nc.sbuf_tensor(name, shape, F32))

    def sem(name):
        return ctx.enter_context(nc.semaphore(name))

    X = sb("X", [128, GROUPS, 32, 2 * WIDTH])
    W = sb("W", [128, 2, KYQ * 2 * KXM * CH])
    XT = sb("XT", [128, 32, 128])
    XP = sb("XP", [128, GROUPS, J, 128])
    T = sb("T", [128, 80 * CH])
    S = sb("S", [128, KYQ, 2, QIMG, KXM, 2])
    G = sb("G", [128, QIMG, KYQ, 2 * MODES])
    GT = sb("GT", [128, TURNS, 4, 4, CH])
    UP = sb("UP", [128, 128, MODES])
    UT = sb("UT", [PACK_K, 2, len(PACKS), 128])
    Y = sb("Y", [128, 2, 512])
    rows_c, spec_c = sb("rows_c", [128, WIDE]), sb("spec_c", [128, 2, 2, WIDE])
    cols_c, pix_c = sb("cols_c", [128, TURN_KYQ, 128]), sb("pix_c", [PACK_K, (PACK + 2) * WIDTH])
    ident = sb("ident", [128, 128])
    conv_w = sb("conv_w", [128, LAYERS, 128])
    conv_b = sb("conv_b", [128, LAYERS])
    lift_w = sb("lift_w", [16, 128])
    lift_t = sb("lift_t", [128, 16])
    conv0_w = sb("conv0_w", [16, 128])
    fc1_w, fc1_b = sb("fc1_w", [128, 2, 128]), sb("fc1_b", [128, 1])
    fc2_w, fc2_b = sb("fc2_w", [128, 2, 32]), sb("fc2_b", [128, 1])
    H = XT[:, :, :].rearrange("p a b -> p (a b)").rearrange("p (s n) -> p s n", s=8)
    T0 = T[:, 0:GROUPS * J * 80].rearrange("p (g n j) -> p g n j", g=GROUPS, j=J)
    T3 = T[:, :].rearrange("p (n c) -> p n c", c=CH)
    SC = G[0:16, :, :, :].rearrange("p i q n -> p (i q n)")
    SC5 = SC.rearrange("p (q r n) -> p q r n", q=KYQ, r=2)
    S4 = S[:, :, :, :, :, :].rearrange("p q r i m c -> p q r (i m c)")
    S_flat = S[:, :, :, :, :, :].rearrange("p q r i m c -> p (q r i m c)")
    UP_flat = UP[:, :, :].rearrange("p n k -> p (n k)")
    XT_flat = XT[:, :, :].rearrange("p a b -> p (a b)")

    z_banks = [ctx.enter_context(nc.psum_tensor(f"z_bank{i}", [128, 512], F32)) for i in range(2)]
    h_banks = [ctx.enter_context(nc.psum_tensor(f"h_bank{i}", [128, 512], F32)) for i in range(2)]
    ring = [ctx.enter_context(nc.psum_tensor(f"ring{i}", [128, 512], F32)) for i in range(BANKS)]

    consts_in, coords_in = sem("consts_in"), sem("coords_in")
    planes_in = [sem(f"planes_in{g}") for g in range(GROUPS)]
    weights_in = [sem("weights_in0"), sem("weights_in1")]
    cleared, ident_made = sem("cleared"), sem("ident_made")
    conv0_filled, conv0_made = sem("conv0_filled"), sem("conv0_made")
    ring_filled, ring_emptied = sem("ring_filled"), sem("ring_emptied")
    z_filled, z_emptied = sem("z_filled"), sem("z_emptied")
    h_filled, h_emptied = sem("h_filled"), sem("h_emptied")
    small_begun = sem("small_begun")
    mixed, coords_used, features_used = sem("mixed"), sem("coords_used"), sem("features_used")
    y_stored, y_free = sem("y_stored"), sem("y_free")

    const_loads = [(rows_c[:, :], d["rows"]), (spec_c[:, :, :, :], d["spec"].rearrange("p (a b n) -> p a b n", a=2, b=2)),
                   (cols_c[:, :, :], d["cols"].rearrange("p (k n) -> p k n", k=TURN_KYQ)),
                   (pix_c[:, :], d["pix"]),
                   (conv_w[:, :, :], d["conv_w"]), (conv_b[:, :], d["conv_b"]),
                   (lift_w[:, :], d["lift_w"]), (lift_t[:, :], d["lift_t"]),
                   (fc1_w[:, :, :], d["fc1_w"]), (fc1_b[:, :], d["fc1_b"]),
                   (fc2_w[:, :, :], d["fc2_w"]), (fc2_b[:, :], d["fc2_b"])]
    Y_STORES = 4
    Y_USES = HEAD_UNITS // 4

    block = ctx.enter_context(nc.Block())

    @block.sync
    def _(sp):
        for dst, src in const_loads:
            sp.dma_start(dst, src).then_inc(consts_in, 16)
        with sp.Fori(0, QUARTERS) as q:
            sp.wait_ge(coords_used, q + 1)
            sp.dma_start(XP[:, :, :, :], d["x_pix"][bass.ds(q, 1), :, :].rearrange("a p (g j m) -> (a p) g j m", g=GROUPS, j=J)) \
              .then_inc(coords_in, 16)
            for layer in range(LAYERS):
                sp.wait_ge(mixed, q * LAYERS + layer + 1)
                sp.dma_start(W[:, layer % 2, :], d["spec_w"][layer, :, :]).then_inc(weights_in[layer % 2], 16)
                if layer == 1:
                    for g in range(GROUPS):
                        sp.wait_ge(features_used, q * GROUPS + g + 1)
                        src = d["x_planes"][bass.ds(q, 1), g, :, :]
                        sp.dma_start(X[0:16, g, :, :], src.rearrange("a p (r w) -> (a p) r w", r=32)) \
                          .then_inc(planes_in[g], 16)

    @block.gpsimd
    def _(pool):
        pool.memset(GT[:, :, :, :, :], 0.0).then_inc(cleared, 1)
        pool.memset(ident[:, :], 0.0).then_inc(ident_made, 1)
        pool.wait_ge(ident_made, 1)
        pool.affine_select(out=ident[:, :], in_=ident[:, :], compare_op=ALU.not_equal, fill=1.0,
                           base=0, pattern=[[-1, 128]], channel_multiplier=1).then_inc(ident_made, 1)
        for slots, count in ((ring_emptied, BANKS), (z_emptied, 2), (h_emptied, 2), (mixed, 2),
                             (coords_used, 1), (features_used, GROUPS), (y_free, 2)):
            pool.sem_inc(slots, count)
        with pool.Fori(0, QUARTERS) as q:
            for n in range(Y_USES):
                g, v = n // 2, n % 2
                pool.wait_ge(ring_emptied, q * RING_USES + BANKS + AFTER[(LAYERS - 1, "fc2", g, v)])
                for c in range(Y_STORES):
                    u = 4 * v + c
                    dst = tok[bass.ds(q * QIMG + 4 * g, 4), :].rearrange("b (h n) -> b h n", h=2)
                    pool.dma_start(dst[:, :, 256 * u:256 * u + 256],
                                   Y[32 * c:32 * c + 4, n % 2, :].rearrange("b (h n) -> b h n", h=2)).then_inc(y_stored, 16)
                pool.wait_ge(y_stored, (q * Y_USES + n + 1) * (16 * Y_STORES))
                pool.sem_inc(y_free, 1)

    @block.tensor
    def _(pe):
        pe.wait_ge(consts_in, 16 * len(const_loads))
        pe.wait_ge(ident_made, 2)
        pe.wait_ge(cleared, 1)
        pe.matmul(z_banks[0][0:16, 0:128], lift_t[:, :], conv_w[:, 0, :], start=True, stop=True).then_inc(conv0_filled, 1)
        pe.wait_ge(conv0_made, 1)

        with pe.Fori(0, QUARTERS) as q:
            z_at = h_at = 0
            for stage in tower_stages():
                layer, kind, a, b = stage
                used = AFTER[stage]
                bank = ring[(used - 1) % BANKS]

                def claim():
                    pe.wait_ge(ring_emptied, q * RING_USES + used)

                def copied(*key):
                    pe.wait_ge(ring_emptied, q * RING_USES + BANKS + AFTER[key])

                if kind == "coord_rows":
                    if a == 0:
                        pe.wait_ge(coords_in, 16 * q + 16)
                    claim()
                    for j in range(J):
                        mm = pe.matmul(bank[:, 80 * j:80 * j + WIDE], XP[:, a, j, :], rows_c[:, :], start=True, stop=True)
                    mm.then_inc(ring_filled, 1)
                elif kind == "coord_spec":
                    copied(0, "coord_rows", a, 0)
                    claim()
                    for kyq in range(KYQ):
                        for r in range(2):
                            at = ((a * 2 + b) * 2 + r) * MODES * J + kyq * 4 * J
                            lhs = T[:, at:at + 4 * J]
                            mm = pe.matmul(bank[0:16, 80 * kyq:80 * kyq + WIDE], lhs, spec_c[:, b, r, :],
                                           start=(r == 0), stop=(r == 1))
                            if a == 0 and b == 0 and kyq == 0 and r == 0:
                                mm.then_inc(coords_used, 1)
                    mm.then_inc(ring_filled, 1)
                elif kind == "lift":
                    if a == 0:
                        copied(0, "coord_spec", GROUPS - 1, 1)
                    claim()
                    pe.matmul(bank[:, 0:400], lift_w[:, :], SC[:, 400 * a:400 * a + 400], start=True, stop=True) \
                      .then_inc(ring_filled, 1)
                elif kind == "mix":
                    if a == 0 and b == 0:
                        if layer == 0:
                            copied(0, "lift", 2 * GROUPS - 1, 0)
                        else:
                            copied(layer - 1, "spec", GROUPS - 1, 1)
                        pe.wait_ge(weights_in[layer % 2], q * 32 + 16 * (layer // 2) + 16)
                    claim()
                    pe.sem_inc(small_begun, 1)
                    for m in range(KXM):
                        at = ((a * 2 + b) * KXM + m) * CH
                        for j in range(4):
                            rows = slice(32 * j, 32 * j + 32)
                            mm = pe.matmul(bank[rows, 32 * m:32 * m + 32], W[rows, layer % 2, at:at + CH],
                                           S[rows, a, b, :, m, :], start=True, stop=True)
                    mm.then_inc(ring_filled, 1)
                elif kind == "turn":
                    if a == 0 and b == 0:
                        copied(layer, "mix", KYQ - 1, 1)
                    claim()
                    pe.sem_inc(small_begun, 1)
                    for k in range(4):
                        src = G[:, 4 * a + k, TURN_KYQ * b:min(KYQ, TURN_KYQ * b + TURN_KYQ), :].rearrange("p q n -> p (q n)")
                        mm = pe.transpose(bank[0:src.shape[1], 128 * k:128 * k + 128], src, ident[:, :])
                        if a == 0 and b == 0 and k == 0:
                            mm.then_inc(mixed, 1)
                    mm.then_inc(ring_filled, 1)
                elif kind == "cols":
                    copied(layer, "turn", a, b // TURN_KYQ)
                    claim()
                    for j in range(4):
                        mm = pe.matmul(bank[:, 128 * j:128 * j + 128], GT[:, b // TURN_KYQ, j, :, :], cols_c[:, b % TURN_KYQ, :], start=True, stop=True)
                    mm.then_inc(ring_filled, 1)
                elif kind == "part":
                    if b == 0:
                        copied(layer, "cols", a, KYQ - 1)
                    claim()
                    for k, (row, _, _, _) in enumerate(PACKS):
                        at = 2 * MODES * (8 * b + row)
                        mm = pe.transpose(bank[0:PACK_K, 128 * k:128 * k + 128], UP_flat[:, at:at + PACK_K], ident[:, :])
                    mm.then_inc(ring_filled, 1)
                elif kind == "z":
                    copied(layer, "part", a, b)
                    if b == 0 and layer == 0:
                        pe.wait_ge(planes_in[a], q * 16 + 16)
                    pe.wait_ge(z_emptied, q * Z_UNITS + z_at + 1)
                    zb = z_banks[z_at % 2]
                    src = X[:, a, 4 * b:4 * b + 4, :]
                    if layer == 0:
                        pe.matmul(zb[:, :], conv0_w[:, :], src[0:16], start=True, stop=False)
                    else:
                        pe.matmul(zb[:, :], conv_w[:, layer, :], src, start=True, stop=False)
                    for k, (_, col, row, n) in enumerate(PACKS):
                        mm = pe.matmul(zb[:, WIDTH * row:WIDTH * (row + n)], UT[:, b % 2, k, :], pix_c[:, col:col + WIDTH * n],
                                       start=False, stop=(k == 2))
                    mm.then_inc(z_filled, 1)
                    z_at += 1
                elif kind == "pix":
                    pe.wait_ge(z_emptied, q * Z_UNITS + 2 + (layer * GROUPS + a) * UNITS + b + 1)
                    claim()
                    for k in range(4):
                        mm = pe.transpose(bank[:, 128 * k:128 * k + 128], X[:, a, 4 * b + k, :], ident[:, :])
                    mm.then_inc(ring_filled, 1)
                elif kind == "rows":
                    if b == 0:
                        copied(layer, "pix", a, UNITS - 1)
                    claim()
                    for i in range(min(6, CH - 6 * b)):
                        lhs = XT_flat[:, 6 * b + i::CH]
                        mm = pe.matmul(bank[:, 80 * i:80 * i + WIDE], lhs, rows_c[:, :], start=True, stop=True)
                    mm.then_inc(ring_filled, 1)
                elif kind == "spec":
                    if b == 0:
                        copied(layer, "rows", a, ROW_USES - 1)
                    claim()
                    for kyq in range(KYQ):
                        for r in range(2):
                            at = (b * 2 + r) * MODES * CH + kyq * 4 * CH
                            lhs = T[:, at:at + 4 * CH]
                            mm = pe.matmul(bank[:, 80 * kyq:80 * kyq + WIDE], lhs, spec_c[:, b, r, :],
                                           start=(r == 0), stop=(r == 1))
                    mm.then_inc(ring_filled, 1)
                elif kind == "fc1":
                    pe.wait_ge(z_emptied, q * Z_UNITS + 2 + (layer * GROUPS + a) * UNITS + b + 1)
                    for pair in range(2):
                        pe.wait_ge(h_emptied, q * (2 * HEAD_UNITS) + h_at + 1)
                        mm = pe.matmul(h_banks[pair][:, :], fc1_w[:, pair, :], X[:, a, 4 * b:4 * b + 4, :],
                                       start=True, stop=True)
                        mm.then_inc(h_filled, 1)
                        h_at += 1
                elif kind == "fc2":
                    pe.wait_ge(h_emptied, q * (2 * HEAD_UNITS) + 2 + 2 * (a * UNITS + 4 * b + 4))
                    claim()
                    for pair in range(2):
                        for c in range(4):
                            mm = pe.matmul(bank[32 * c:32 * c + 32, :], fc2_w[:, pair, :], H[:, 2 * c + pair, :],
                                           start=(pair == 0), stop=(pair == 1))
                            if b == 1 and pair == 0 and c == 0:
                                mm.then_inc(features_used, 1)
                    mm.then_inc(ring_filled, 1)

    @block.scalar
    def _(act):
        act.wait_ge(consts_in, 16 * len(const_loads))
        with act.Fori(0, QUARTERS) as q:
            z_at = h_at = 0
            for layer, kind, a, b in tower_stages():
                if kind == "z":
                    act.wait_ge(z_filled, q * Z_UNITS + z_at + 1)
                    act.activation(X[:, a, 4 * b:4 * b + 4, :], z_banks[z_at % 2][:, :].rearrange("p (r w) -> p r w", r=4),
                                   ACT.Gelu, bias=conv_b[:, layer:layer + 1]).then_inc(z_emptied, 1)
                    z_at += 1
                elif kind == "fc1":
                    for pair in range(2):
                        act.wait_ge(h_filled, q * (2 * HEAD_UNITS) + h_at + 1)
                        act.activation(H[:, h_at % 8, :], h_banks[pair][:, :], ACT.Gelu,
                                       bias=fc1_b[:, 0:1]).then_inc(h_emptied, 1)
                        h_at += 1

    @block.vector
    def _(dve):
        dve.wait_ge(conv0_filled, 1)
        dve.tensor_copy(conv0_w[:, :], z_banks[0][0:16, 0:128]).then_inc(conv0_made, 1)
        dve.wait_ge(consts_in, 16 * len(const_loads))
        dve.wait_ge(cleared, 1)
        with dve.Fori(0, QUARTERS) as q:
            y_at = 0
            for stage in tower_stages():
                layer, kind, a, b = stage
                if not in_ring(stage):
                    continue
                bank = ring[(AFTER[stage] - 1) % BANKS]
                dve.wait_ge(ring_filled, q * RING_USES + AFTER[stage])
                if kind == "coord_rows":
                    copy = dve.tensor_copy(T0[:, a, :, :].rearrange("p n j -> p j n"), bank[:, 0:320].rearrange("p (j n) -> p j n", j=J))
                elif kind == "coord_spec":
                    dst = SC5.rearrange("p q r (g n) -> p g r q n", g=GROUPS)[:, a, b, :, :]
                    copy = dve.tensor_copy(dst, bank[0:16, 0:400].rearrange("p (q n) -> p q n", q=KYQ))
                elif kind == "lift":
                    copy = dve.tensor_copy(S_flat[:, 400 * a:400 * a + 400], bank[:, 0:400])
                elif kind == "mix":
                    dst = G[:, :, a, 20 * b:20 * b + 20].rearrange("p i (m c) -> p i m c", c=2)
                    copy = dve.tensor_copy(dst, bank[:, 0:320].rearrange("p (m i c) -> p i m c", m=KXM, c=2))
                elif kind == "turn":
                    rows = 2 * MODES * min(TURN_KYQ, KYQ - TURN_KYQ * b)
                    copy = dve.tensor_copy(GT[0:rows, b, :, :, :].rearrange("p j k o -> p k j o"),
                                           bank[0:rows, :].rearrange("p (k j o) -> p k j o", k=4, j=4))
                elif kind == "cols":
                    copy = dve.tensor_copy(UP[:, :, 4 * b:4 * b + 4].rearrange("p n j -> p j n"),
                                           bank[:, :].rearrange("p (j n) -> p j n", j=4))
                elif kind == "part":
                    copy = dve.tensor_copy(UT[:, b % 2, :, :], bank[0:PACK_K, 0:384].rearrange("p (k n) -> p k n", k=3))
                elif kind == "pix":
                    copy = dve.tensor_copy(XT[:, 4 * b:4 * b + 4, :], bank[:, :].rearrange("p (r n) -> p r n", r=4))
                elif kind == "rows":
                    n = min(6, CH - 6 * b)
                    copy = dve.tensor_copy(T3[:, :, 6 * b:6 * b + n].rearrange("p n c -> p c n"),
                                           bank[:, 0:80 * n].rearrange("p (c n) -> p c n", n=80))
                elif kind == "spec":
                    dst = S4.rearrange("p q r (g n) -> p g r q n", g=GROUPS)[:, a, b, :, :]
                    copy = dve.tensor_copy(dst, bank[:, 0:400].rearrange("p (q n) -> p q n", q=KYQ))
                else:
                    dve.wait_ge(y_free, q * Y_USES + y_at + 1)
                    copy = dve.tensor_scalar(Y[:, y_at % 2, :].rearrange("p (h r w) -> p r h w", h=2, w=WIDTH),
                                             bank[:, :].rearrange("p (r h w) -> p r h w", r=4, h=2),
                                             fc2_b[:, 0:1], None, ALU.add)
                    y_at += 1
                copy.then_inc(ring_emptied, 1)


TILES = IMAGES * HEIGHT // 128 // QUARTERS
C = WIDTH
EXPERTS, EHID = 32, 16
HEADS = 8
FHID, FEXPERTS = 256, 8
LN_EPS = 1e-5
ATT_EPS = 1e-6
TBANKS = 7
NORMS = 6


def token_stages():
    for kind, n in (("xT", 2), ("qT", 2), ("kv", 2), ("outer", 4), ("msg", 4), ("msgT", 2), ("merge", 1),
                    ("catT", 2), ("up", 2), ("down", 1), ("routeT", 2), ("route", 1)):
        for a in range(n):
            yield kind, a
    for t in range(TILES + 1):
        if t < TILES:
            yield "hidden", t
        if t >= 1:
            yield "hiddenT", t - 1
    yield "pickT", 0
    yield "expert", 0
    for kind, n in (("attnT", 2), ("q4", 8), ("k4", 2), ("v4", 2)):
        for a in range(n):
            yield kind, a
    for t in range(TILES + 2):
        if t < TILES:
            yield "score", t
        if t >= 2:
            yield "blend", t - 2
    yield "attend", 0
    for kind, n in (("ffnT", 2), ("ffn1", 4), ("gate", 1), ("gateT", 1), ("ffn2", TILES), ("ffnb", 1)):
        for a in range(n):
            yield kind, a


TOKEN_USES = sum(1 for _ in token_stages())
TOKEN_AFTER = {s: n + 1 for n, s in enumerate(token_stages())}
assert TOKEN_USES % TBANKS == 0


def tokens(nc, ctx, d, tok, out):
    def sb(name, shape):
        return ctx.enter_context(nc.sbuf_tensor(name, shape, F32))

    def sem(name):
        return ctx.enter_context(nc.semaphore(name))

    names = {}
    loads = []
    for name in ("wq1", "wkv", "headmask", "wm", "w1", "w2", "g1", "b1", "g2", "b2", "rw", "ew1", "ew2", "eb2",
                 "rev32", "rev8", "wq4", "wk4", "wv4", "wo4", "fw1", "fwg", "bg", "fwd", "fbd"):
        names[name] = sb("t_" + name, list(d[name].shape))
        loads.append((names[name], d[name]))
    wq1, wkv, headmask, wm, w1, w2 = (names[n] for n in ("wq1", "wkv", "headmask", "wm", "w1", "w2"))
    rw, ew1, ew2, eb2 = (names[n] for n in ("rw", "ew1", "ew2", "eb2"))
    wq4, wk4, wv4, wo4 = (names[n] for n in ("wq4", "wk4", "wv4", "wo4"))
    fw1, fwg, bg, fwd, fbd = (names[n] for n in ("fw1", "fwg", "bg", "fwd", "fbd"))
    rev32, rev8 = names["rev32"], names["rev8"]

    ident = sb("t_ident", [128, 128])
    eps = sb("eps", [128, 1])
    h = sb("h", [128, TILES, C])
    cat = sb("cat", [128, TILES, 2 * C])
    ext = sb("ext", [128, TILES, 128])
    xT = sb("xT", [128, TILES * 128])
    centered, squared = sb("centered", [128, TILES, C]), sb("squared", [128, TILES, C])
    mean, var, std, rstd = (sb(n, [128, TILES]) for n in ("mean", "var", "std", "rstd"))
    wide0, wide1 = sb("wide0", [128, TILES, C]), sb("wide1", [128, TILES, C])
    q_raw, q_exp = sb("q_raw", [64, TILES * 128]), sb("q_exp", [64, TILES * 128])
    Q = sb("Q", [128, TILES * 128])
    k_raw, k_exp, K = (sb(n, [128, TILES, C]) for n in ("k_raw", "k_exp", "K"))
    V = sb("V", [128, TILES, 2, 128])
    KV = sb("KV", [128, TILES, 2, 128])
    den = sb("den", [128, TILES, C])
    upT = sb("upT", [128, TILES * 128])
    logits, hit = sb("logits", [128, TILES, EXPERTS]), sb("hit", [128, TILES, EXPERTS])
    pick = sb("pick", [128, TILES, EXPERTS])
    top, first = sb("top", [128, TILES]), sb("first", [128, TILES])
    pickT = sb("pickT", [128, 2, 128])
    hidden = sb("hidden", [128, 2, EXPERTS * EHID])
    hiddenT = sb("hiddenT", [128, TILES, 4, 128])
    q4 = sb("q4", [128, 4, TILES * 128])
    K4 = sb("K4", [128, 2 * TILES, 2, 64])
    V4 = sb("V4", [128, 2 * TILES, 64])
    attn = sb("attn", [128, 3, HEADS, 64])
    total = sb("total", [128, HEADS])
    peak, scale = (sb(n, [128, 2, HEADS]) for n in ("peak", "scale"))
    blend = sb("blend", [128, TILES, 2, 64])
    fT = sb("fT", [128, 2, TILES * 128])
    gl, ge, gp, gh, gw = (sb(n, [128, TILES, FEXPERTS]) for n in ("gl", "ge", "gp", "gh", "gw"))
    gtop, gsum, grec = (sb(n, [128, TILES]) for n in ("gtop", "gsum", "grec"))
    gwT = sb("gwT", [128, 128])
    chosen = sb("chosen", [128, FEXPERTS, 64])
    ffn = sb("ffn", [128, TILES, C])
    result = sb("result", [128, TILES, C])
    banks = [ctx.enter_context(nc.psum_tensor(f"t_bank{i}", [128, 512], F32)) for i in range(TBANKS)]

    weights_in, h_in, stored = sem("weights_in"), sem("h_in"), sem("stored")
    h_free = sem("h_free")
    result_free = sem("result_free")
    t_ready = sem("t_ready")
    filled, emptied = sem("filled"), sem("emptied")
    is_centered, has_var, normed = sem("is_centered"), sem("has_var"), sem("normed")
    q_ready, k_ready, msg_ready, picked = sem("q_ready"), sem("k_ready"), sem("msg_ready"), sem("picked")
    attn_ready, gate_logits, gate_ready, result_ready = sem("attn_ready"), sem("gate_logits"), sem("gate_ready"), sem("result_ready")
    dve_step = sem("dve_step")
    is_squared, has_std = sem("is_squared"), sem("has_std")
    act_step, q_exped, k_exped, exped, gate_exped, gelued = (sem(n) for n in ("act_step", "q_exped", "k_exped", "exped", "gate_exped", "gelued"))
    small_begun2 = sem("small_begun2")
    READY = 13

    block = ctx.enter_context(nc.Block())

    @block.sync
    def _(sp):
        for dst, src in loads:
            full = tuple(slice(None) for _ in dst.shape)
            sp.dma_start(dst[full], src).then_inc(weights_in, 16)
        tok_v = tok.rearrange("(q t p) c -> q p t c", q=QUARTERS, p=128)
        with sp.Fori(0, QUARTERS) as c:
            sp.wait_ge(h_free, c + 1)
            sp.dma_start(h[:, :, :], tok_v[bass.ds(c, 1), :, :, :].rearrange("a p t c -> (a p) t c")).then_inc(h_in, 16)

    @block.gpsimd
    def _(pool):
        zeros = (ident[:, :], cat[:, :, :], ext[:, :, :], V[:, :, :, :], Q[:, :], KV[:, :, :, :], K4[:, :, :, :], gwT[:, :])
        for zero in zeros:
            pool.memset(zero, 0.0).then_inc(t_ready, 1)
        pool.memset(eps[:, :], LN_EPS).then_inc(t_ready, 1)
        pool.wait_ge(t_ready, 9)
        pool.affine_select(out=ident[:, :], in_=ident[:, :], compare_op=ALU.not_equal, fill=1.0,
                           base=0, pattern=[[-1, 128]], channel_multiplier=1).then_inc(t_ready, 1)
        pool.wait_ge(t_ready, 10)
        pool.memset(ext[:, :, C:C + 1], 1.0).then_inc(t_ready, 1)
        pool.wait_ge(t_ready, 11)
        pool.memset(V[0:64, :, 0, 64:128], 1.0).then_inc(t_ready, 1)
        pool.wait_ge(t_ready, 12)
        pool.memset(V[64:128, :, 1, 64:128], 1.0).then_inc(t_ready, 1)
        pool.sem_inc(emptied, TBANKS)
        pool.sem_inc(result_free, 1)
        pool.sem_inc(h_free, 1)
        out_v = out.rearrange("(q t p) c -> q p t c", q=QUARTERS, p=128)
        with pool.Fori(0, QUARTERS) as c:
            pool.wait_ge(result_ready, c + 1)
            pool.sem_inc(h_free, 1)
            pool.dma_start(out_v[bass.ds(c, 1), :, :, :].rearrange("a p t c -> (a p) t c"), result[:, :, :]).then_inc(stored, 16)
            pool.wait_ge(stored, 16 * c + 16)
            pool.sem_inc(result_free, 1)

    @block.tensor
    def _(pe):
        pe.wait_ge(weights_in, 16 * len(loads))
        pe.wait_ge(t_ready, READY)
        with pe.Fori(0, QUARTERS) as c:
            for kind, a in token_stages():
                used = TOKEN_AFTER[(kind, a)]
                bank = banks[(used - 1) % TBANKS]

                def copied(*key):
                    pe.wait_ge(emptied, c * TOKEN_USES + TBANKS + TOKEN_AFTER[key])

                def by_tile(n, step, width, terms):
                    for t in range(n):
                        wd = width if step * t + width <= 512 else step
                        for k, (lhs, r) in enumerate(terms(t)):
                            mm = pe.matmul(bank[:, step * t:step * t + wd], lhs, r[:, 0:wd], start=(k == 0), stop=(k == len(terms(t)) - 1))
                    return mm

                first = {"xT": ("normed", 1), "catT": ("normed", 2), "routeT": ("normed", 4), "attnT": ("normed", 5), "ffnT": ("normed", 6)}
                if kind in first and a == 0:
                    pe.wait_ge(normed, c * NORMS + first[kind][1])
                if kind == "msgT" and a == 0:
                    copied("msg", 3)
                if kind == "qT":
                    copied("xT", a)
                if kind == "kv" and a == 0:
                    copied("xT", 1)
                if kind == "outer" and a == 0:
                    pe.wait_ge(k_ready, c + 1)
                    copied("kv", 1)
                if kind == "msg":
                    if a == 0:
                        pe.wait_ge(q_ready, c + 1)
                    copied("outer", a)
                if kind == "merge":
                    copied("msgT", 1)
                if kind == "up":
                    copied("catT", a)
                if kind == "down":
                    copied("up", 1)
                if kind == "route":
                    copied("routeT", 1)
                if kind == "hiddenT":
                    copied("hidden", a)
                if kind == "pickT":
                    pe.wait_ge(picked, c + 1)
                if kind == "expert":
                    copied("pickT", 0)
                if kind == "q4" and a < 2:
                    copied("attnT", a)
                if kind == "score" and a == 0:
                    copied("k4", 1)
                if kind == "blend":
                    pe.wait_ge(attn_ready, c * TILES + a + 1)
                if kind == "attend":
                    copied("blend", TILES - 1)
                if kind == "ffn1" and a < 2:
                    copied("ffnT", a)
                if kind == "gate":
                    pe.wait_ge(gelued, c * 4 + 4)
                if kind == "gateT":
                    pe.wait_ge(gate_ready, c + 1)
                if kind == "ffnb":
                    copied("gateT", 0)
                pe.wait_ge(emptied, c * TOKEN_USES + used)

                if kind in ("xT", "msgT", "catT", "routeT", "attnT", "ffnT"):
                    src = cat if kind in ("xT", "msgT", "catT") else ext
                    for k in range(4):
                        mm = pe.transpose(bank[:, 128 * k:128 * k + 128], src[:, 4 * a + k, :], ident[:, :])
                elif kind == "qT":
                    mm = pe.matmul(bank[0:64, :], wq1[:, :], xT[:, 512 * a:512 * a + 512], start=True, stop=True)
                elif kind == "kv":
                    for k in range(4):
                        t = 4 * a + k
                        mm = pe.matmul(bank[:, 128 * k:128 * k + 128], xT[:, 128 * t:128 * t + 128], wkv[:, :], start=True, stop=True)
                elif kind == "outer":
                    for k in range(2):
                        t = 2 * a + k
                        mm = pe.matmul(bank[0:64, 256 * k:256 * k + 256], K[:, t, :], V[:, t, :, :], start=True, stop=True)
                elif kind == "msg":
                    for k in range(2):
                        t = 2 * a + k
                        mm = pe.matmul(bank[:, 256 * k:256 * k + 256], Q[:, 128 * t:128 * t + 128], KV[:, t, :, :], start=True, stop=True)
                elif kind == "merge":
                    mm = by_tile(TILES, C, WIDE, lambda t: [(xT[:, 128 * t:128 * t + 128], wm)])
                elif kind == "up":
                    mm = pe.matmul(bank[:, :], w1[:, :], xT[:, 512 * a:512 * a + 512], start=True, stop=True)
                elif kind == "down":
                    mm = by_tile(TILES, C, WIDE, lambda t: [(upT[:, 128 * t:128 * t + 128], w2)])
                elif kind == "route":
                    mm = by_tile(TILES, EXPERTS, WIDE, lambda t: [(xT[:, 128 * t:128 * t + 128], rw)])
                elif kind == "hidden":
                    mm = pe.matmul(bank[:, :], xT[:, 128 * a:128 * a + 128], ew1[:, :], start=True, stop=True)
                elif kind == "hiddenT":
                    for k in range(4):
                        mm = pe.transpose(bank[:, 128 * k:128 * k + 128], hidden[:, a % 2, 128 * k:128 * k + 128], ident[:, :])
                elif kind == "pickT":
                    for k in range(2):
                        mm = pe.transpose(bank[:, 128 * k:128 * k + 128], pick[:, 4 * k:4 * k + 4, :], ident[:, :])
                elif kind == "expert":
                    mm = by_tile(TILES, C, WIDE, lambda t: [(hiddenT[:, t, k, :], ew2[:, k, :]) for k in range(4)]
                                 + [(pickT[:, t // 4, :], eb2[:, t % 4, :])])
                elif kind == "q4":
                    p, n = a // 2, a % 2
                    mm = pe.matmul(bank[:, :], wq4[:, p, :], xT[:, 512 * n:512 * n + 512], start=True, stop=True)
                elif kind == "k4":
                    mm = pe.matmul(bank[:, :], wk4[:, :], xT[:, 512 * a:512 * a + 512], start=True, stop=True)
                elif kind == "v4":
                    mm = pe.matmul(bank[:, :], wv4[:, :], xT[:, 512 * a:512 * a + 512], start=True, stop=True)
                elif kind == "score":
                    for p in range(4):
                        for i in range(2):
                            img = 2 * a + i
                            mm = pe.matmul(bank[64 * i:64 * i + 64, 128 * p:128 * p + 128], q4[:, p, 64 * img:64 * img + 64],
                                           K4[:, img, :, :], start=True, stop=True)
                elif kind == "blend":
                    for p in range(4):
                        for odd in range(2):
                            mm = pe.matmul(bank[64 * odd:64 * odd + 64, 0:128], attn[:, a % 3, 2 * p + odd, :], wo4[:, 2 * p + odd, :],
                                           start=(p == 0), stop=(p == 3))
                elif kind == "attend":
                    for t in range(TILES):
                        for i in range(2):
                            mm = pe.matmul(bank[64 * i:64 * i + 64, 64 * t:64 * t + 64], V4[:, 2 * t + i, :], blend[:, t, i, :],
                                           start=True, stop=True)
                elif kind == "ffn1":
                    half, n = a // 2, a % 2
                    mm = pe.matmul(bank[:, :], fw1[:, 128 * half:128 * half + 128], xT[:, 512 * n:512 * n + 512], start=True, stop=True)
                elif kind == "gate":
                    mm = by_tile(TILES, FEXPERTS, WIDE, lambda t: [(fT[:, k, 128 * t:128 * t + 128], fwg[:, k, :]) for k in range(2)])
                elif kind == "gateT":
                    pe.sem_inc(small_begun2, 1)
                    mm = pe.transpose(bank[0:64, 0:128], gw[:, :, :], ident[:, :])
                elif kind == "ffn2":
                    for k in range(2):
                        mm = pe.matmul(bank[:, :], fT[:, k, 128 * a:128 * a + 128], fwd[:, k, :], start=(k == 0), stop=(k == 1))
                elif kind == "ffnb":
                    mm = by_tile(TILES, C, WIDE, lambda t: [(gwT[:, :], fbd[:, t, :])])
                mm.then_inc(filled, 1)

    @block.scalar
    def _(act):
        act.wait_ge(t_ready, READY)
        steps = [0]
        ACT_STEPS = 2

        with act.Fori(0, QUARTERS) as c:
            def taken(*key):
                act.wait_ge(emptied, c * TOKEN_USES + TBANKS + TOKEN_AFTER[key])

            def norm(n):
                act.wait_ge(is_centered, c * NORMS + n + 1)
                act.activation(squared[:, :, :], centered[:, :, :], ACT.Square).then_inc(is_squared, 1)
                act.wait_ge(has_var, c * NORMS + n + 1)
                act.activation(std[:, :], var[:, :], ACT.Sqrt, bias=eps[:, 0:1], scale=1.0 / C).then_inc(has_std, 1)

            def exp_below_zero(dst, src, done):
                act.activation(dst, src, ACT.Relu, scale=-1.0).then_inc(act_step, 1)
                steps[0] += 1
                act.wait_ge(act_step, c * ACT_STEPS + steps[0])
                act.activation(dst, dst, ACT.Exp, scale=-1.0).then_inc(done, 1)

            norm(0)
            taken("qT", 1)
            exp_below_zero(q_exp[:, :], q_raw[:, :], q_exped)
            taken("kv", 1)
            exp_below_zero(k_exp[:, :, :], k_raw[:, :, :], k_exped)
            for n in range(1, 5):
                norm(n)
            for t in range(TILES):
                taken("score", t)
                act.activation(attn[:, t % 3, :, :], attn[:, t % 3, :, :], ACT.Exp, scale=8.0 ** -0.5).then_inc(exped, 1)
            norm(5)
            for k in range(4):
                taken("ffn1", k)
                part = fT[:, k // 2, 512 * (k % 2):512 * (k % 2) + 512]
                act.activation(part, part, ACT.Gelu).then_inc(gelued, 1)
            act.wait_ge(gate_logits, c + 1)
            act.activation(ge[:, :, :], ge[:, :, :], ACT.Exp).then_inc(gate_exped, 1)

    @block.vector
    def _(dve):
        dve.wait_ge(weights_in, 16 * len(loads))
        dve.wait_ge(t_ready, READY)
        DVE_STEPS = 71
        with dve.Fori(0, QUARTERS) as c:
            steps = [0]

            def link(ins):
                ins.then_inc(dve_step, 1)
                steps[0] += 1
                dve.wait_ge(dve_step, c * DVE_STEPS + steps[0])

            def bank_of(kind, a):
                dve.wait_ge(filled, c * TOKEN_USES + TOKEN_AFTER[(kind, a)])
                return banks[(TOKEN_AFTER[(kind, a)] - 1) % TBANKS]

            def taken(kind, a):
                dve.wait_ge(emptied, c * TOKEN_USES + TBANKS + TOKEN_AFTER[(kind, a)])

            def wide(ap, n):
                return ap.unsqueeze(2).to_broadcast([128, ap.shape[1], n])

            def norm(n, src, dst, gain=None, shift=None):
                link(dve.tensor_reduce(mean[:, :], src, AX.X, ALU.add))
                dve.scalar_tensor_tensor(out=centered[:, :, :], in0=wide(mean[:, :], C), scalar=-1.0 / C, in1=src,
                                         op0=ALU.mult, op1=ALU.add).then_inc(is_centered, 1)
                dve.wait_ge(is_squared, c * NORMS + n + 1)
                dve.tensor_reduce(var[:, :], squared[:, :, :], AX.X, ALU.add).then_inc(has_var, 1)
                dve.wait_ge(has_std, c * NORMS + n + 1)
                link(dve.reciprocal(rstd[:, :], std[:, :]))
                if gain is None:
                    dve.tensor_tensor(dst, centered[:, :, :], wide(rstd[:, :], C), ALU.mult).then_inc(normed, 1)
                    return
                link(dve.tensor_tensor(centered[:, :, :], centered[:, :, :], wide(rstd[:, :], C), ALU.mult))
                rows = [128, TILES, C]
                link(dve.tensor_tensor(centered[:, :, :], centered[:, :, :], gain[:, :].unsqueeze(1).to_broadcast(rows), ALU.mult))
                dve.tensor_tensor(dst, centered[:, :, :], shift[:, :].unsqueeze(1).to_broadcast(rows), ALU.add).then_inc(normed, 1)

            def turned(kind):
                for n in range(2):
                    b = bank_of(kind, n)
                    dve.tensor_copy(xT[:, 512 * n:512 * n + 512], b[:, :]).then_inc(emptied, 1)

            dve.wait_ge(h_in, 16 * c + 16)
            norm(0, h[:, :, :], cat[:, :, 0:C])
            turned("xT")
            for n in range(2):
                b = bank_of("qT", n)
                dve.tensor_copy(q_raw[:, 512 * n:512 * n + 512], b[0:64, :]).then_inc(emptied, 1)
            for n in range(2):
                b = bank_of("kv", n)[:, :].rearrange("p (t k) -> p t k", t=4)
                four = slice(4 * n, 4 * n + 4)
                dve.tensor_copy(k_raw[:, four, :], b[:, :, 0:64])
                dve.tensor_copy(V[0:64, four, 0, 0:64], b[0:64, :, 64:128])
                dve.tensor_copy(V[64:128, four, 1, 0:64], b[64:128, :, 64:128]).then_inc(emptied, 1)
            dve.wait_ge(q_exped, c + 1)
            dve.scalar_tensor_tensor(out=Q[0:64, :], in0=q_raw[:, :], scalar=0.0, in1=q_exp[:, :], op0=ALU.max, op1=ALU.add).then_inc(q_ready, 1)
            dve.wait_ge(k_exped, c + 1)
            dve.scalar_tensor_tensor(out=K[:, :, :], in0=k_raw[:, :, :], scalar=0.0, in1=k_exp[:, :, :], op0=ALU.max, op1=ALU.add).then_inc(k_ready, 1)
            for n in range(4):
                b = bank_of("outer", n)[0:64, :].rearrange("p (t i k) -> p (t i) k", t=2, i=2)
                dst = KV[0:64, 2 * n:2 * n + 2, :, :].rearrange("p t i k -> p (t i) k")
                dve.tensor_tensor(dst, b, headmask[:, :].unsqueeze(1).to_broadcast([64, 4, 128]), ALU.mult).then_inc(emptied, 1)
            for n in range(4):
                b = bank_of("msg", n)[:, :].rearrange("p (t i k) -> p t i k", t=2, i=2)
                two = slice(2 * n, 2 * n + 2)
                dve.tensor_scalar(den[0:64, two, :], b[0:64, :, 0, 64:128], ATT_EPS, None, ALU.add)
                link(dve.tensor_scalar(den[64:128, two, :], b[64:128, :, 1, 64:128], ATT_EPS, None, ALU.add))
                link(dve.reciprocal(den[:, two, :], den[:, two, :]))
                dve.tensor_tensor(cat[0:64, two, C:2 * C], b[0:64, :, 0, 0:64], den[0:64, two, :], ALU.mult)
                dve.tensor_tensor(cat[64:128, two, C:2 * C], b[64:128, :, 1, 0:64], den[64:128, two, :], ALU.mult).then_inc(emptied, 1)
            turned("msgT")
            b = bank_of("merge", 0)
            dve.tensor_copy(wide0[:, :, :], b[:, :].rearrange("p (t k) -> p t k", t=TILES)).then_inc(emptied, 1)
            taken("merge", 0)
            norm(1, wide0[:, :, :], cat[:, :, C:2 * C], names["g1"], names["b1"])
            turned("catT")
            for n in range(2):
                b = bank_of("up", n)
                dve.tensor_scalar(upT[:, 512 * n:512 * n + 512], b[:, :], 0.0, None, ALU.max).then_inc(emptied, 1)
            b = bank_of("down", 0)
            dve.tensor_copy(wide0[:, :, :], b[:, :].rearrange("p (t k) -> p t k", t=TILES)).then_inc(emptied, 1)
            taken("down", 0)
            norm(2, wide0[:, :, :], wide1[:, :, :], names["g2"], names["b2"])
            dve.wait_ge(normed, c * NORMS + 3)
            link(dve.tensor_tensor(wide1[:, :, :], wide1[:, :, :], cat[:, :, 0:C], ALU.add))
            link(dve.tensor_tensor(h[:, :, :], h[:, :, :], wide1[:, :, :], ALU.add))

            norm(3, h[:, :, :], ext[:, :, 0:C])
            turned("routeT")
            b = bank_of("route", 0)
            dve.tensor_copy(logits[:, :, :], b[:, 0:TILES * EXPERTS].rearrange("p (t e) -> p t e", t=TILES)).then_inc(emptied, 1)
            taken("route", 0)
            link(dve.tensor_reduce(top[:, :], logits[:, :, :], AX.X, ALU.max))
            link(dve.tensor_tensor(hit[:, :, :], logits[:, :, :], wide(top[:, :], EXPERTS), ALU.is_equal))
            link(dve.tensor_tensor(hit[:, :, :], hit[:, :, :], rev32[:, :].unsqueeze(1).to_broadcast([128, TILES, EXPERTS]), ALU.mult))
            link(dve.tensor_reduce(first[:, :], hit[:, :, :], AX.X, ALU.max))
            dve.tensor_tensor(pick[:, :, :], hit[:, :, :], wide(first[:, :], EXPERTS), ALU.is_equal).then_inc(picked, 1)
            dve.wait_ge(picked, c + 1)
            for t in range(TILES + 1):
                if t < TILES:
                    b = bank_of("hidden", t)[:, :].rearrange("p (e k) -> p e k", e=EXPERTS)
                    dst = hidden[:, t % 2, :].rearrange("p (e k) -> p e k", e=EXPERTS)
                    dve.scalar_tensor_tensor(out=dst, in0=b, scalar=0.0, in1=wide(pick[:, t, :], EHID), op0=ALU.max, op1=ALU.mult).then_inc(emptied, 1)
                if t >= 1:
                    b = bank_of("hiddenT", t - 1)
                    dve.tensor_copy(hiddenT[:, t - 1, :, :], b[:, :].rearrange("p (k n) -> p k n", k=4)).then_inc(emptied, 1)
            b = bank_of("pickT", 0)
            dve.tensor_copy(pickT[:, :, :], b[:, 0:256].rearrange("p (k n) -> p k n", k=2)).then_inc(emptied, 1)
            b = bank_of("expert", 0)
            dve.scalar_tensor_tensor(out=h[:, :, :], in0=b[:, :].rearrange("p (t k) -> p t k", t=TILES), scalar=0.0, in1=h[:, :, :],
                                     op0=ALU.max, op1=ALU.add).then_inc(emptied, 1)
            taken("expert", 0)

            norm(4, h[:, :, :], ext[:, :, 0:C])
            turned("attnT")
            for a in range(8):
                p, n = a // 2, a % 2
                b = bank_of("q4", a)
                dve.tensor_copy(q4[:, p, 512 * n:512 * n + 512], b[:, :]).then_inc(emptied, 1)
            for n in range(2):
                b = bank_of("k4", n)[:, :].rearrange("p (i t) -> p i t", i=8)
                dve.tensor_copy(K4[0:64, 8 * n:8 * n + 8, 0, :], b[0:64, :, :])
                dve.tensor_copy(K4[64:128, 8 * n:8 * n + 8, 1, :], b[64:128, :, :]).then_inc(emptied, 1)
            for n in range(2):
                b = bank_of("v4", n)
                dve.tensor_copy(V4[:, 8 * n:8 * n + 8, :], b[:, :].rearrange("p (i k) -> p i k", i=8)).then_inc(emptied, 1)
            for t in range(TILES + 2):
                if t < TILES:
                    b = bank_of("score", t)[:, :].rearrange("p (h t) -> p h t", h=HEADS)
                    link(dve.tensor_reduce(peak[:, t % 2, :], b, AX.X, ALU.max))
                    dve.tensor_tensor(attn[:, t % 3, :, :], b, wide(peak[:, t % 2, :], 64), ALU.subtract).then_inc(emptied, 1)
                if 1 <= t <= TILES:
                    dve.wait_ge(exped, c * TILES + t)
                    a = attn[:, (t - 1) % 3, :, :]
                    link(dve.tensor_reduce(total[:, :], a, AX.X, ALU.add))
                    link(dve.reciprocal(scale[:, t % 2, :], total[:, :]))
                    dve.tensor_tensor(a, a, wide(scale[:, t % 2, :], 64), ALU.mult).then_inc(attn_ready, 1)
                if t >= 2:
                    b = bank_of("blend", t - 2)
                    dve.tensor_copy(blend[:, t - 2, :, :], b[:, 0:128].rearrange("p (i k) -> p i k", i=2)).then_inc(emptied, 1)
            b = bank_of("attend", 0)
            dve.tensor_tensor(h[:, :, :], b[:, :].rearrange("p (t k) -> p t k", t=TILES), h[:, :, :], ALU.add).then_inc(emptied, 1)
            taken("attend", 0)

            norm(5, h[:, :, :], ext[:, :, 0:C])
            turned("ffnT")
            for a in range(4):
                b = bank_of("ffn1", a)
                dve.tensor_copy(fT[:, a // 2, 512 * (a % 2):512 * (a % 2) + 512], b[:, :]).then_inc(emptied, 1)
            b = bank_of("gate", 0)
            dve.tensor_tensor(gl[:, :, :], b[:, 0:TILES * FEXPERTS].rearrange("p (t e) -> p t e", t=TILES),
                              bg[:, :].unsqueeze(1).to_broadcast([128, TILES, FEXPERTS]), ALU.add).then_inc(emptied, 1)
            taken("gate", 0)
            link(dve.tensor_reduce(gtop[:, :], gl[:, :, :], AX.X, ALU.max))
            dve.tensor_tensor(ge[:, :, :], gl[:, :, :], wide(gtop[:, :], FEXPERTS), ALU.subtract).then_inc(gate_logits, 1)
            dve.wait_ge(gate_exped, c + 1)
            link(dve.tensor_reduce(gsum[:, :], ge[:, :, :], AX.X, ALU.add))
            link(dve.reciprocal(grec[:, :], gsum[:, :]))
            link(dve.tensor_tensor(gp[:, :, :], ge[:, :, :], wide(grec[:, :], FEXPERTS), ALU.mult))
            link(dve.tensor_reduce(gtop[:, :], gp[:, :, :], AX.X, ALU.max))
            link(dve.tensor_tensor(gh[:, :, :], gp[:, :, :], wide(gtop[:, :], FEXPERTS), ALU.is_equal))
            link(dve.tensor_tensor(gh[:, :, :], gh[:, :, :], rev8[:, :].unsqueeze(1).to_broadcast([128, TILES, FEXPERTS]), ALU.mult))
            link(dve.tensor_reduce(gsum[:, :], gh[:, :, :], AX.X, ALU.max))
            link(dve.tensor_tensor(gh[:, :, :], gh[:, :, :], wide(gsum[:, :], FEXPERTS), ALU.is_equal))
            dve.tensor_tensor(gw[:, :, :], gh[:, :, :], gp[:, :, :], ALU.mult).then_inc(gate_ready, 1)
            dve.wait_ge(gate_ready, c + 1)
            b = bank_of("gateT", 0)
            dve.tensor_copy(gwT[0:64, :], b[0:64, 0:128]).then_inc(emptied, 1)
            for t in range(TILES):
                b = bank_of("ffn2", t)[:, :].rearrange("p (e k) -> p e k", e=FEXPERTS)
                dve.tensor_tensor(chosen[:, :, :], b, wide(gw[:, t, :], 64), ALU.mult).then_inc(emptied, 1)
                taken("ffn2", t)
                link(dve.tensor_reduce(ffn[:, t, :], chosen[:, :, :].rearrange("p e k -> p k e"), AX.X, ALU.add))
            b = bank_of("ffnb", 0)
            dve.tensor_tensor(wide0[:, :, :], b[:, :].rearrange("p (t k) -> p t k", t=TILES), h[:, :, :], ALU.add).then_inc(emptied, 1)
            taken("ffnb", 0)
            dve.wait_ge(result_free, c + 1)
            dve.tensor_tensor(result[:, :, :], wide0[:, :, :], ffn[:, :, :], ALU.add).then_inc(result_ready, 1)
            assert steps[0] == DVE_STEPS, steps[0]


def program(nc, d, out):
    with ExitStack() as ctx:
        tok = nc.dram_tensor("tok", (IMAGES, PIX), F32, kind="Internal").ap()
        tower(nc, ctx, d, tok)
    with ExitStack() as ctx:
        tokens(nc, ctx, d, tok.rearrange("b (s c) -> (b s) c", c=C), out.rearrange("b s c -> (b s) c"))


_OUTS = [((64, 64, 64), 'float32')]


def block_diagonal(a, n):
    out = np.zeros((n, a.shape[0], n, a.shape[1]), a.dtype)
    for i in range(n):
        out[i, :, i, :] = a
    return out.reshape(n * a.shape[0], n * a.shape[1])


def lay_out(x):
    f = np.float32
    one = np.ones((IMAGES, HEIGHT, WIDTH, 1), f)
    xa = np.concatenate([x["x"], one], axis=-1).reshape(QUARTERS, GROUPS, 4, 2, 32, WIDTH, J)
    fc0 = np.concatenate([x["L0_tok_fc0_w"], x["L0_tok_fc0_b"][None]], axis=0)
    sw = np.stack([x[f"L0_tok_sw{i}"] for i in range(LAYERS)])
    conv = [block_diagonal(x[f"L0_tok_cw{i}"].T, 4) for i in range(LAYERS)]
    fc1 = np.zeros((128, 2, 128), f)
    fc2 = np.zeros((128, 2, 32), f)
    for pair in range(2):
        fc1[64 * pair:64 * pair + 64, pair] = block_diagonal(x["L0_tok_fc1_w"], 2)
        fc2[:, pair, 2 * pair:2 * pair + 2] = block_diagonal(x["L0_tok_fc2_w"], 2)
    out = {
        "x_planes": xa.transpose(0, 1, 2, 6, 4, 3, 5).reshape(QUARTERS, GROUPS, 16, PIX),
        "x_pix": xa.transpose(0, 3, 5, 1, 6, 4, 2).reshape(QUARTERS, 128, GROUPS * J * 128),
        "spec_w": sw.reshape(LAYERS, CH, CH, KXM, 2, KYQ, 4).transpose(0, 6, 1, 5, 4, 3, 2).reshape(LAYERS, 128, -1),
        "conv_w": np.stack(conv, axis=1),
        "conv_b": np.stack([np.tile(x[f"L0_tok_cb{i}"], 4) for i in range(LAYERS)], axis=1),
        "lift_w": block_diagonal(fc0, 4), "lift_t": block_diagonal(fc0.T, 4),
        "fc1_w": fc1, "fc1_b": np.tile(x["L0_tok_fc1_b"], 2)[:, None],
        "fc2_w": fc2, "fc2_b": np.full((128, 1), x["L0_tok_fc2_b"][0]),
    }
    out.update(fourier_tables())

    def below(a, columns=0, rows=128, at=0):
        b = np.zeros((rows,) + a.shape[1:-1] + (max(columns, a.shape[-1]),), f)
        b[at:at + a.shape[0], ..., :a.shape[-1]] = a
        return b

    def with_bias(w, b):
        return np.concatenate([w, b[None]], axis=0)

    heads = np.arange(64) // 8
    rep = lambda v: np.tile(v[None], (128, 1))
    wq4 = x["L1_attn_Wq"].reshape(4, 128, 64).transpose(2, 0, 1)
    wo = x["L1_attn_Wo"].reshape(64, 64, 8).transpose(1, 2, 0)
    wo4 = np.zeros((2, 64, 8, 2, 64), f)
    wo4[0, :, :, 0], wo4[1, :, :, 1] = wo, wo
    eb2 = np.zeros((4, 32, 4, WIDE), f)
    fbd = np.zeros((16, 8, 8, WIDE), f)
    for t in range(4):
        eb2[t, :, t, :64] = x["L0_ffn_b2"]
    for t in range(8):
        fbd[t, :, t, :64] = x["L1_ffn_bd"]
    wk, wv = x["L1_attn_Wk"].T, x["L1_attn_Wv"].T
    out.update({
        "wq1": below(x["L0_attn_Wq"]), "wkv": below(np.concatenate([x["L0_attn_Wk"], x["L0_attn_Wv"]], axis=1)),
        "headmask": np.tile((heads[:, None] == heads[None, :]).astype(f), (1, 2)),
        "wm": below(x["L0_attn_Wm"], WIDE, at=64), "w1": x["L0_attn_W1"], "w2": below(x["L0_attn_W2"], WIDE),
        "g1": rep(x["L0_attn_g1"]), "b1": rep(x["L0_attn_b1"]), "g2": rep(x["L0_attn_g2"]), "b2": rep(x["L0_attn_b2"]),
        "rw": below(with_bias(x["L0_ffn_router_w"].T, x["L0_ffn_router_b"]), WIDE),
        "ew1": below(with_bias(x["L0_ffn_W1"].transpose(1, 0, 2).reshape(64, 512), x["L0_ffn_b1"].reshape(512))),
        "ew2": below(x["L0_ffn_W2"].reshape(4, 128, 64).transpose(1, 0, 2), WIDE), "eb2": eb2.reshape(128, 4, WIDE),
        "rev32": rep(np.arange(32, 0, -1).astype(f)), "rev8": rep(np.arange(8, 0, -1).astype(f)),
        "wq4": below(wq4), "wk4": below(np.concatenate([wk, wk], axis=1)), "wv4": below(np.concatenate([wv, wv], axis=1)),
        "wo4": wo4.reshape(128, 8, 128),
        "fw1": below(with_bias(x["L1_ffn_W1"], x["L1_ffn_b1"])),
        "fwg": below(x["L1_ffn_Wg"].reshape(2, 128, 8).transpose(1, 0, 2), WIDE), "bg": rep(x["L1_ffn_bg"]),
        "fwd": x["L1_ffn_Wd"].transpose(1, 0, 2).reshape(2, 128, 512).transpose(1, 0, 2), "fbd": fbd.reshape(128, 8, WIDE),
    })
    return {k: np.ascontiguousarray(v) for k, v in out.items()}


def kernel(**inputs):
    import concourse.bacc as _bacc
    from concourse.bass_utils import run_bass_kernel_spmd as _run

    nc = _bacc.Bacc("TRN2", target_bir_lowering=False, num_devices=1)
    laid = lay_out({k: np.asarray(v) for k, v in inputs.items()})
    d = {k: nc.dram_tensor(f"in_{k}", v.shape, mybir.dt.from_np(v.dtype), kind="ExternalInput").ap() for k, v in laid.items()}
    out = nc.dram_tensor("out_0", (64, 64, 64), F32, kind="ExternalOutput").ap()
    program(nc, d, out)
    r = _run(nc, [{f"in_{k}": v for k, v in laid.items()}], core_ids=[0])
    return r.results[0]["out_0"]
```

```python
from contextlib import ExitStack

import numpy as np
import concourse.bass as bass
from concourse import mybir

F32 = mybir.dt.float32
F32R = mybir.dt.float32r
ALU = mybir.AluOpType
ACT = mybir.ActivationFunctionType
AX = mybir.AxisListType

IMAGES, HEIGHT, WIDTH = 64, 64, 64
CH = 32
MODES = 20
LAYERS = 4
HID = 64
J = 4
QUARTERS = 4
QIMG = IMAGES // QUARTERS
GROUPS = QIMG // 4
PIX = HEIGHT * WIDTH
UNITS = 8
KYQ = MODES // 4
KXM = MODES // 2
TURN_KYQ = 3
TURNS = -(-KYQ // TURN_KYQ)
ROW_USES = 6
PACK = 3
PACK_K = PACK * 2 * MODES
PACKS = ((0, 0, 0, 3), (3, 0, 3, 3), (5, PACK * WIDTH, 6, 2))
WIDE = 96
BANKS = 4


def tower_stages():
    for g in range(GROUPS):
        yield 0, "coord_rows", g, 0
    for n in range(GROUPS // 2):
        yield 0, "coord_spec", n, 0
    for kyq in range(KYQ):
        for p in range(2):
            yield 0, "lift", kyq, p
    for layer in range(LAYERS):
        last = layer == LAYERS - 1
        for kyq in range(KYQ):
            yield layer, "mix", kyq, 0
            yield layer, "mix", kyq, 1
        for part in range(TURNS):
            yield layer, "turn", 0, part
        for n in range(4 * TURNS):
            yield layer, "cols", 0, n
        yield layer, "split", 0, 0
        yield layer, "part", 0, 0
        for g in range(GROUPS):
            for u in range(UNITS):
                before = (g, u - 1) if u >= 1 else (g - 1, UNITS - 1)
                if last and before[0] >= 0:
                    yield layer, "head_split", *before
                if u + 1 < UNITS:
                    yield layer, "part", g, u + 1
                    yield layer, "split", g, u + 1
                if g + 1 < GROUPS and 1 <= u <= TURNS:
                    yield layer, "turn", g + 1, u - 1
                yield layer, "z", g, u
                if g + 1 < GROUPS and u >= 6:
                    for n in range(4):
                        yield layer, "cols", g + 1, 4 * (u - 6) + n
                    if u == 6:
                        yield layer, "split", g + 1, 0
                if last:
                    if u == 5:
                        yield layer, "fc2", g, 0
                    if u == 1 and g >= 1:
                        yield layer, "fc2", g - 1, 1
                    if before[0] >= 0:
                        yield layer, "fc1", *before
                    continue
                if g >= 1 and u < 2:
                    yield layer, "pix", g - 1, UNITS - 2 + u
                if g >= 1 and u == 2:
                    for n in range(ROW_USES):
                        yield layer, "rows", g - 1, n
                if u >= 2:
                    yield layer, "pix", g, u - 2
                if g >= 1 and u == 4:
                    yield layer, "spec", g - 1, 0
                    yield layer, "spec", g - 1, 1
            if last and g == GROUPS - 1:
                yield layer, "head_split", g, UNITS - 1
                yield layer, "fc1", g, UNITS - 1
            if g + 1 < GROUPS:
                yield layer, "part", g + 1, 0
        if last:
            yield layer, "fc2", GROUPS - 1, 1
        else:
            g = GROUPS - 1
            yield layer, "pix", g, UNITS - 2
            yield layer, "pix", g, UNITS - 1
            for n in range(ROW_USES):
                yield layer, "rows", g, n
            yield layer, "spec", g, 0
            yield layer, "spec", g, 1


def in_ring(stage):
    return stage[1] not in ("z", "fc1", "split", "head_split")


RING_USES = sum(in_ring(s) for s in tower_stages())
Z_UNITS = LAYERS * GROUPS * UNITS
HEAD_UNITS = GROUPS * UNITS
assert RING_USES % BANKS == 0
SPLITS = sum(s[1] in ("turn", "split", "head_split") for s in tower_stages())
PRODUCTS = ((0, 0), (0, 1), (1, 0))


def ring_counts():
    at, out = 0, {}
    for s in tower_stages():
        at += in_ring(s)
        out[s] = at
    return out


AFTER = ring_counts()


def fourier_tables():
    t64 = 2 * np.pi / 64
    w = np.arange(64)
    rows = np.zeros((2, 64, 2, 2, MODES))
    for p in range(2):
        for h1 in range(2):
            sign = (-1.0) ** (p * h1)
            a = t64 * np.outer(w, np.arange(MODES))
            rows[h1, :, p, 0, :] = sign * np.cos(a)
            rows[h1, :, p, 1, :] = -sign * np.sin(a)
    spec = np.zeros((32, 4, 2, 2, 4, KXM, 2))
    for b in range(4):
        for p in range(2):
            a = t64 * np.outer(np.arange(32), 2 * np.arange(KXM) + p)
            spec[:, b, p, 0, b, :, 0] = np.cos(a) / 64
            spec[:, b, p, 0, b, :, 1] = -np.sin(a) / 64
            spec[:, b, p, 1, b, :, 0] = np.sin(a) / 64
            spec[:, b, p, 1, b, :, 1] = np.cos(a) / 64
    cols = np.zeros((128, TURN_KYQ, 32, 2, 2))
    h = np.arange(32)[:, None] + 32 * np.arange(2)[None, :]
    for p in range(2):
        for m in range(KXM):
            a = t64 * (2 * m + p) * h
            for k in range(TURN_KYQ):
                r = k * 2 * MODES + (p * KXM + m) * 2
                cols[r, k, :, :, 0], cols[r + 1, k, :, :, 0] = np.cos(a), -np.sin(a)
                cols[r, k, :, :, 1], cols[r + 1, k, :, :, 1] = np.sin(a), np.cos(a)
    pix = np.zeros((PACK, 2, MODES, PACK + 2, 64))
    for ky in range(MODES):
        c = (1.0 if ky == 0 else 2.0) / 64
        for row in range(PACK):
            for to in (row, PACK + row - 1)[:1 if row == 0 else 2]:
                pix[row, 0, ky, to] = c * np.cos(t64 * ky * w)
                pix[row, 1, ky, to] = -c * np.sin(t64 * ky * w)
    f = np.float32
    wide = ((0, 0), (0, 0), (0, WIDE - 80))
    return {"rows": np.pad(rows.reshape(128, 1, 80), wide).reshape(128, WIDE).astype(f),
            "spec": np.pad(spec.reshape(128, 4, 80), wide).reshape(128, 4 * WIDE).astype(f),
            "cols": cols.reshape(128, TURN_KYQ * 128).astype(f), "pix": pix.reshape(PACK_K, (PACK + 2) * WIDTH).astype(f)}


def tower(nc, ctx, d, tok):
    def sb(name, shape):
        return ctx.enter_context(nc.sbuf_tensor(name, shape, F32))

    def sem(name):
        return ctx.enter_context(nc.semaphore(name))

    X = sb("X", [128, GROUPS, 32, 2 * WIDTH])
    W = sb("W", [128, 2, KYQ * 2 * KXM * CH])
    XT = sb("XT", [128, 32, 128])
    XP = sb("XP", [128, GROUPS, J, 128])
    T = sb("T", [128, 80 * CH])
    S = sb("S", [128, KYQ, 2, QIMG, KXM, 2])
    G = sb("G", [128, QIMG, KYQ, 2 * MODES])
    GT = ctx.enter_context(nc.sbuf_tensor("GT", [128, 2, TURNS, 4, 4, CH], F32R))
    UP = sb("UP", [128, 128, MODES])
    UT = sb("UT", [PACK_K, 2, len(PACKS), 128])
    Y = sb("Y", [128, 2, 512])
    XS = ctx.enter_context(nc.sbuf_tensor("XS", [128, 2, 2, 512], F32R))
    HS = ctx.enter_context(nc.sbuf_tensor("HS", [128, 2, 2, 512], F32R))
    conv_r = ctx.enter_context(nc.sbuf_tensor("conv_r", [128, 2, LAYERS, 128], F32R))
    fc1_r = ctx.enter_context(nc.sbuf_tensor("fc1_r", [128, 2, 2, 128], F32R))
    rows_c, spec_c = sb("rows_c", [128, WIDE]), sb("spec_c", [128, 2, 2, WIDE])
    cols_c = ctx.enter_context(nc.sbuf_tensor("cols_c", [128, 2, TURN_KYQ * 128], F32R))
    pix_c = sb("pix_c", [PACK_K, (PACK + 2) * WIDTH])
    ident = sb("ident", [128, 128])
    conv_b = sb("conv_b", [128, LAYERS])
    lift_w = sb("lift_w", [MODES * J, KYQ, 128])
    lift_t = sb("lift_t", [128, 16])
    conv0_w = ctx.enter_context(nc.sbuf_tensor("conv0_w", [16, 2, 128], F32R))
    fc1_b = sb("fc1_b", [128, 1])
    fc2_w, fc2_b = sb("fc2_w", [128, 2, 32]), sb("fc2_b", [128, 1])
    H = XT[:, :, :].rearrange("p a b -> p (a b)").rearrange("p (s n) -> p s n", s=8)
    T0 = T[:, 0:GROUPS * J * 80].rearrange("p (g n j) -> p g n j", g=GROUPS, j=J)
    T3 = T[:, :].rearrange("p (n c) -> p n c", c=CH)
    G_flat = G[:, :, :, :].rearrange("p i q n -> p (i q n)")
    wholes = [cols_w, fc1_w, conv_w] = [G_flat[:, 0:384], G_flat[:, 384:640], G_flat[:, 640:1152]]
    SC = G_flat[0:MODES * J, 0:2 * GROUPS * 80].rearrange("p (r n) -> p r n", r=2)
    S4 = S[:, :, :, :, :, :].rearrange("p q r i m c -> p q r (i m c)")
    UP_flat = UP[:, :, :].rearrange("p n k -> p (n k)")
    XT_flat = XT[:, :, :].rearrange("p a b -> p (a b)")

    z_banks = [ctx.enter_context(nc.psum_tensor(f"z_bank{i}", [128, 512], F32)) for i in range(2)]
    h_banks = [ctx.enter_context(nc.psum_tensor(f"h_bank{i}", [128, 512], F32)) for i in range(2)]
    ring = [ctx.enter_context(nc.psum_tensor(f"ring{i}", [128, 512], F32)) for i in range(BANKS)]

    consts_in, coords_in = sem("consts_in"), sem("coords_in")
    planes_in = [sem(f"planes_in{g}") for g in range(GROUPS)]
    weights_in = [sem("weights_in0"), sem("weights_in1")]
    cleared, ident_made = sem("cleared"), sem("ident_made")
    conv0_filled, conv0_made = sem("conv0_filled"), sem("conv0_made")
    ring_filled, ring_emptied = sem("ring_filled"), sem("ring_emptied")
    z_filled, z_emptied = sem("z_filled"), sem("z_emptied")
    h_filled, h_emptied = sem("h_filled"), sem("h_emptied")
    small_begun, high_made = sem("small_begun"), sem("high_made")
    weights_split, x_split, head_split = sem("weights_split"), sem("x_split"), sem("head_split")
    mixed, coords_used, features_used = sem("mixed"), sem("coords_used"), sem("features_used")
    y_stored, y_free = sem("y_stored"), sem("y_free")

    const_loads = [(rows_c[:, :], d["rows"]), (spec_c[:, :, :, :], d["spec"].rearrange("p (a b n) -> p a b n", a=2, b=2)),
                   (cols_w, d["cols"]),
                   (pix_c[:, :], d["pix"]),
                   (conv_w, d["conv_w"].rearrange("p l n -> p (l n)")), (conv_b[:, :], d["conv_b"]),
                   (lift_w[:, :, :], d["lift_w"].rearrange("p (q n) -> p q n", q=KYQ)), (lift_t[:, :], d["lift_t"]),
                   (fc1_w, d["fc1_w"].rearrange("p a n -> p (a n)")), (fc1_b[:, :], d["fc1_b"]),
                   (fc2_w[:, :, :], d["fc2_w"]), (fc2_b[:, :], d["fc2_b"])]
    Y_STORES = 4
    Y_USES = HEAD_UNITS // 4

    block = ctx.enter_context(nc.Block())

    @block.sync
    def _(sp):
        for dst, src in const_loads:
            sp.dma_start(dst, src).then_inc(consts_in, 16)
        with sp.Fori(0, QUARTERS) as q:
            sp.wait_ge(coords_used, q + 1)
            sp.dma_start(XP[:, :, :, :], d["x_pix"][bass.ds(q, 1), :, :].rearrange("a p (g j m) -> (a p) g j m", g=GROUPS, j=J)) \
              .then_inc(coords_in, 16)
            for layer in range(LAYERS):
                sp.wait_ge(mixed, q * LAYERS + layer + 1)
                sp.dma_start(W[:, layer % 2, :], d["spec_w"][layer, :, :]).then_inc(weights_in[layer % 2], 16)
                if layer == 1:
                    for g in range(GROUPS):
                        sp.wait_ge(features_used, q * GROUPS + g + 1)
                        src = d["x_planes"][bass.ds(q, 1), g, :, :]
                        sp.dma_start(X[0:16, g, :, :], src.rearrange("a p (r w) -> (a p) r w", r=32)) \
                          .then_inc(planes_in[g], 16)

    @block.gpsimd
    def _(pool):
        pool.memset(XT_flat[:, 0:2048], 0.0).then_inc(cleared, 1)
        pool.memset(ident[:, :], 0.0).then_inc(ident_made, 1)
        pool.wait_ge(ident_made, 1)
        pool.affine_select(out=ident[:, :], in_=ident[:, :], compare_op=ALU.not_equal, fill=1.0,
                           base=0, pattern=[[-1, 128]], channel_multiplier=1).then_inc(ident_made, 1)
        for slots, count in ((ring_emptied, BANKS), (z_emptied, 2), (h_emptied, 2), (mixed, 2),
                             (coords_used, 1), (features_used, GROUPS), (y_free, 2)):
            pool.sem_inc(slots, count)
        with pool.Fori(0, QUARTERS) as q:
            for n in range(Y_USES):
                g, v = n // 2, n % 2
                pool.wait_ge(ring_emptied, q * RING_USES + BANKS + AFTER[(LAYERS - 1, "fc2", g, v)])
                for c in range(Y_STORES):
                    u = 4 * v + c
                    dst = tok[bass.ds(q * QIMG + 4 * g, 4), :].rearrange("b (h n) -> b h n", h=2)
                    pool.dma_start(dst[:, :, 256 * u:256 * u + 256],
                                   Y[32 * c:32 * c + 4, n % 2, :].rearrange("b (h n) -> b h n", h=2)).then_inc(y_stored, 16)
                pool.wait_ge(y_stored, (q * Y_USES + n + 1) * (16 * Y_STORES))
                pool.sem_inc(y_free, 1)

    @block.tensor
    def _(pe):
        pe.wait_ge(consts_in, 16 * len(const_loads))
        pe.wait_ge(ident_made, 2)
        pe.wait_ge(cleared, 1)
        pe.matmul(z_banks[0][0:16, 0:128], lift_t[:, :], conv_w[:, 0:128], start=True, stop=True).then_inc(conv0_filled, 1)
        pe.wait_ge(conv0_made, 2)
        pe.wait_ge(weights_split, 7)

        with pe.Fori(0, QUARTERS) as q:
            z_at = h_at = 0
            for stage in tower_stages():
                layer, kind, a, b = stage
                used = AFTER[stage]
                bank = ring[(used - 1) % BANKS]

                def claim():
                    pe.wait_ge(ring_emptied, q * RING_USES + used)

                def copied(*key):
                    pe.wait_ge(ring_emptied, q * RING_USES + BANKS + AFTER[key])

                if kind == "coord_rows":
                    if a == 0:
                        pe.wait_ge(coords_in, 16 * q + 16)
                    claim()
                    for j in range(J):
                        mm = pe.matmul(bank[:, 80 * j:80 * j + WIDE], XP[:, a, j, :], rows_c[:, :], start=True, stop=True)
                    mm.then_inc(ring_filled, 1)
                elif kind == "coord_spec":
                    copied(0, "coord_rows", 2 * a + 1, 0)
                    claim()
                    for n in range(4):
                        g, p = 2 * a + n // 2, n % 2
                        for r in range(2):
                            at = ((g * 2 + p) * 2 + r) * MODES * J
                            mm = pe.matmul(bank[0:MODES * J, 80 * n:80 * n + WIDE], T[:, at:at + MODES * J], spec_c[:, p, r, :],
                                           start=(r == 0), stop=(r == 1))
                            if a == 1 and n == 0 and r == 0:
                                mm.then_inc(coords_used, 1)
                    mm.then_inc(ring_filled, 1)
                elif kind == "lift":
                    if a == 0 and b == 0:
                        copied(0, "coord_spec", GROUPS // 2 - 1, 0)
                    claim()
                    mm = pe.matmul(bank[:, 0:320], lift_w[:, a, :], SC[:, b, :], start=True, stop=True)
                    mm.then_inc(ring_filled, 1)
                elif kind == "mix":
                    if a == 0 and b == 0:
                        if layer == 0:
                            copied(0, "lift", KYQ - 1, 1)
                        else:
                            copied(layer - 1, "spec", GROUPS - 1, 1)
                        pe.wait_ge(weights_in[layer % 2], q * 32 + 16 * (layer // 2) + 16)
                    claim()
                    pe.sem_inc(small_begun, 1)
                    for m in range(KXM):
                        at = ((a * 2 + b) * KXM + m) * CH
                        for j in range(4):
                            rows = slice(32 * j, 32 * j + 32)
                            mm = pe.matmul(bank[rows, 32 * m:32 * m + 32], W[rows, layer % 2, at:at + CH],
                                           S[rows, a, b, :, m, :], start=True, stop=True)
                    mm.then_inc(ring_filled, 1)
                elif kind == "turn":
                    if a == 0 and b == 0:
                        copied(layer, "mix", KYQ - 1, 1)
                    claim()
                    pe.sem_inc(small_begun, 1)
                    for k in range(4):
                        src = G[:, 4 * a + k, TURN_KYQ * b:min(KYQ, TURN_KYQ * b + TURN_KYQ), :].rearrange("p q n -> p (q n)")
                        mm = pe.transpose(bank[0:src.shape[1], 128 * k:128 * k + 128], src, ident[:, :])
                        if a == 0 and b == 0 and k == 0:
                            mm.then_inc(mixed, 1)
                    mm.then_inc(ring_filled, 1)
                elif kind == "cols":
                    turn, j = b // 4, b % 4
                    copied(layer, "turn", a, turn)
                    claim()
                    n = 128 * min(TURN_KYQ, KYQ - TURN_KYQ * turn)
                    for k, (data, table) in enumerate(PRODUCTS):
                        mm = pe.matmul(bank[:, 0:n], GT[:, data, turn, j, :, :], cols_c[:, table, 0:n], start=(k == 0), stop=(k == 2))
                    mm.then_inc(ring_filled, 1)
                elif kind == "part":
                    if b == 0:
                        copied(layer, "cols", a, 4 * TURNS - 1)
                    claim()
                    for k, (row, _, _, _) in enumerate(PACKS):
                        at = 2 * MODES * (8 * b + row)
                        mm = pe.transpose(bank[0:PACK_K, 128 * k:128 * k + 128], UP_flat[:, at:at + PACK_K], ident[:, :])
                    mm.then_inc(ring_filled, 1)
                elif kind == "z":
                    copied(layer, "part", a, b)
                    pe.wait_ge(z_emptied, q * Z_UNITS + z_at + 1)
                    zb = z_banks[z_at % 2]
                    pe.wait_ge(x_split, q * Z_UNITS + (layer * GROUPS + a) * UNITS + b + 1)
                    for k, (data, weight) in enumerate(PRODUCTS):
                        lhs, rhs = conv_r[:, weight, layer, :], XS[:, b % 2, data, :]
                        if layer == 0:
                            lhs, rhs = conv0_w[:, weight, :], rhs[0:16]
                        pe.matmul(zb[:, :], lhs, rhs, start=(k == 0), stop=False)
                    for k, (_, col, row, n) in enumerate(PACKS):
                        mm = pe.matmul(zb[:, WIDTH * row:WIDTH * (row + n)], UT[:, b % 2, k, :], pix_c[:, col:col + WIDTH * n],
                                       start=False, stop=(k == 2))
                    mm.then_inc(z_filled, 1)
                    z_at += 1
                elif kind == "pix":
                    pe.wait_ge(z_emptied, q * Z_UNITS + 2 + (layer * GROUPS + a) * UNITS + b + 1)
                    claim()
                    for k in range(4):
                        mm = pe.transpose(bank[:, 128 * k:128 * k + 128], X[:, a, 4 * b + k, :], ident[:, :])
                    mm.then_inc(ring_filled, 1)
                elif kind == "rows":
                    if b == 0:
                        copied(layer, "pix", a, UNITS - 1)
                    claim()
                    for i in range(min(6, CH - 6 * b)):
                        lhs = XT_flat[:, 6 * b + i::CH]
                        mm = pe.matmul(bank[:, 80 * i:80 * i + WIDE], lhs, rows_c[:, :], start=True, stop=True)
                    mm.then_inc(ring_filled, 1)
                elif kind == "spec":
                    if b == 0:
                        copied(layer, "rows", a, ROW_USES - 1)
                    claim()
                    for kyq in range(KYQ):
                        for r in range(2):
                            at = (b * 2 + r) * MODES * CH + kyq * 4 * CH
                            lhs = T[:, at:at + 4 * CH]
                            mm = pe.matmul(bank[:, 80 * kyq:80 * kyq + WIDE], lhs, spec_c[:, b, r, :],
                                           start=(r == 0), stop=(r == 1))
                    mm.then_inc(ring_filled, 1)
                elif kind == "fc1":
                    pe.wait_ge(head_split, q * HEAD_UNITS + a * UNITS + b + 1)
                    for pair in range(2):
                        pe.wait_ge(h_emptied, q * (2 * HEAD_UNITS) + h_at + 1)
                        for k, (data, weight) in enumerate(PRODUCTS):
                            mm = pe.matmul(h_banks[pair][:, :], fc1_r[:, weight, pair, :], HS[:, b % 2, data, :],
                                           start=(k == 0), stop=(k == 2))
                        mm.then_inc(h_filled, 1)
                        h_at += 1
                elif kind == "fc2":
                    pe.wait_ge(h_emptied, q * (2 * HEAD_UNITS) + 2 + 2 * (a * UNITS + 4 * b + 4))
                    claim()
                    for pair in range(2):
                        for c in range(4):
                            mm = pe.matmul(bank[32 * c:32 * c + 32, :], fc2_w[:, pair, :], H[:, 2 * c + pair, :],
                                           start=(pair == 0), stop=(pair == 1))
                            if b == 1 and pair == 0 and c == 0:
                                mm.then_inc(features_used, 1)
                    mm.then_inc(ring_filled, 1)

    @block.scalar
    def _(act):
        act.wait_ge(consts_in, 16 * len(const_loads))
        with act.Fori(0, QUARTERS) as q:
            z_at = h_at = 0
            for layer, kind, a, b in tower_stages():
                if kind == "z":
                    act.wait_ge(z_filled, q * Z_UNITS + z_at + 1)
                    act.activation(X[:, a, 4 * b:4 * b + 4, :], z_banks[z_at % 2][:, :].rearrange("p (r w) -> p r w", r=4),
                                   ACT.Gelu, bias=conv_b[:, layer:layer + 1]).then_inc(z_emptied, 1)
                    z_at += 1
                elif kind == "fc1":
                    for pair in range(2):
                        act.wait_ge(h_filled, q * (2 * HEAD_UNITS) + h_at + 1)
                        act.activation(H[:, h_at % 8, :], h_banks[pair][:, :], ACT.Gelu,
                                       bias=fc1_b[:, 0:1]).then_inc(h_emptied, 1)
                        h_at += 1

    @block.vector
    def _(dve):
        dve.wait_ge(conv0_filled, 1)
        dve.tensor_copy(conv0_w[:, 0, :], z_banks[0][0:16, 0:128]).then_inc(conv0_made, 1)
        dve.wait_ge(conv0_made, 1)
        dve.tensor_tensor(conv0_w[:, 1, :], z_banks[0][0:16, 0:128], conv0_w[:, 0, :], ALU.subtract).then_inc(conv0_made, 1)
        dve.wait_ge(consts_in, 16 * len(const_loads))
        parts = [t.rearrange("p s a n -> p s (a n)") if len(t.shape) == 4 else t for t in (cols_c[:, :, :], fc1_r[:, :, :, :], conv_r[:, :, :, :])]
        for whole, part in zip(wholes, parts):
            dve.tensor_copy(part[:, 0, :], whole).then_inc(weights_split, 1)
        dve.wait_ge(weights_split, 3)
        for whole, part in zip(wholes, parts):
            dve.tensor_tensor(part[:, 1, :], whole, part[:, 0, :], ALU.subtract).then_inc(weights_split, 1)
        dve.wait_ge(cleared, 1)
        dve.tensor_copy(GT[:, :, :, :, :, :].rearrange("p s t j b o -> p (s t j b o)"), XT_flat[:, 0:2048]).then_inc(weights_split, 1)
        dve.wait_ge(weights_split, 7)
        with dve.Fori(0, QUARTERS) as q:
            y_at = splits = 0
            for stage in tower_stages():
                layer, kind, a, b = stage

                def split(src, high, low):
                    nonlocal splits
                    dve.tensor_copy(high, src).then_inc(high_made, 1)
                    splits += 1
                    dve.wait_ge(high_made, q * SPLITS + splits)
                    return dve.tensor_tensor(low, src, high, ALU.subtract)

                if kind in ("split", "head_split"):
                    rows = slice(0, 128)
                    if kind == "split" and layer == 0:
                        rows = slice(0, 16)
                        dve.wait_ge(planes_in[a], q * 16 + 16)
                    else:
                        of = layer - 1 if kind == "split" else layer
                        dve.wait_ge(z_emptied, q * Z_UNITS + 2 + (of * GROUPS + a) * UNITS + b + 1)
                    to, done = (XS, x_split) if kind == "split" else (HS, head_split)
                    unit = X[rows, a, 4 * b:4 * b + 4, :].rearrange("p r w -> p (r w)")
                    split(unit, to[rows, b % 2, 0, :], to[rows, b % 2, 1, :]).then_inc(done, 1)
                if not in_ring(stage):
                    continue
                bank = ring[(AFTER[stage] - 1) % BANKS]
                dve.wait_ge(ring_filled, q * RING_USES + AFTER[stage])
                if kind == "coord_rows":
                    copy = dve.tensor_copy(T0[:, a, :, :].rearrange("p n j -> p j n"), bank[:, 0:320].rearrange("p (j n) -> p j n", j=J))
                elif kind == "coord_spec":
                    dst = SC[:, :, 160 * a:160 * a + 160].rearrange("p r (g n) -> p g r n", g=2)
                    copy = dve.tensor_copy(dst, bank[0:MODES * J, 0:320].rearrange("p (g r n) -> p g r n", g=2, r=2))
                elif kind == "lift":
                    copy = dve.tensor_copy(S4[:, a, b, :], bank[:, 0:320])
                elif kind == "mix":
                    dst = G[:, :, a, 20 * b:20 * b + 20].rearrange("p i (m c) -> p i m c", c=2)
                    copy = dve.tensor_copy(dst, bank[:, 0:320].rearrange("p (m i c) -> p i m c", m=KXM, c=2))
                elif kind == "turn":
                    rows = 2 * MODES * min(TURN_KYQ, KYQ - TURN_KYQ * b)
                    src = bank[0:rows, :].rearrange("p (k j o) -> p k j o", k=4, j=4)
                    high, low = (GT[0:rows, part, b, :, :, :].rearrange("p j k o -> p k j o") for part in range(2))
                    copy = split(src, high, low)
                elif kind == "cols":
                    n = min(TURN_KYQ, KYQ - TURN_KYQ * (b // 4))
                    dst = UP[:, :, 4 * TURN_KYQ * (b // 4) + b % 4::4][:, :, 0:n]
                    copy = dve.tensor_copy(dst.rearrange("p n k -> p k n"), bank[:, 0:128 * n].rearrange("p (k n) -> p k n", k=n))
                elif kind == "part":
                    copy = dve.tensor_copy(UT[:, b % 2, :, :], bank[0:PACK_K, 0:384].rearrange("p (k n) -> p k n", k=3))
                elif kind == "pix":
                    copy = dve.tensor_copy(XT[:, 4 * b:4 * b + 4, :], bank[:, :].rearrange("p (r n) -> p r n", r=4))
                elif kind == "rows":
                    n = min(6, CH - 6 * b)
                    copy = dve.tensor_copy(T3[:, :, 6 * b:6 * b + n].rearrange("p n c -> p c n"),
                                           bank[:, 0:80 * n].rearrange("p (c n) -> p c n", n=80))
                elif kind == "spec":
                    dst = S4.rearrange("p q r (g n) -> p g r q n", g=GROUPS)[:, a, b, :, :]
                    copy = dve.tensor_copy(dst, bank[:, 0:400].rearrange("p (q n) -> p q n", q=KYQ))
                else:
                    dve.wait_ge(y_free, q * Y_USES + y_at + 1)
                    copy = dve.tensor_scalar(Y[:, y_at % 2, :].rearrange("p (h r w) -> p r h w", h=2, w=WIDTH),
                                             bank[:, :].rearrange("p (r h w) -> p r h w", r=4, h=2),
                                             fc2_b[:, 0:1], None, ALU.add)
                    y_at += 1
                copy.then_inc(ring_emptied, 1)


TILES = IMAGES * HEIGHT // 128 // QUARTERS
STREAMS = 2
TS = TILES // STREAMS
NT = TS * 128
C = WIDTH
EXPERTS, EHID = 32, 16
HEADS = 8
FEXPERTS = 8
LN_EPS = 1e-5
ATT_EPS = 1e-6
NORMS = 6
D_BANKS, A_BANKS = 2, 2
ACT_TAKES = ("xT", "msgT", "catT", "up", "routeT", "hiddenT", "attnT", "q4", "v4", "ffnT", "ffn1")
NO_BANK = ("norm", "scale", "pick", "soft", "gates", "result")
NORM_BEFORE = {"xT": 1, "catT": 2, "routeT": 4, "attnT": 5, "ffnT": 6}


def stream_stages():
    for kind, a in (("norm", 0), ("scale", 0), ("xT", 0), ("qT", 0), ("kv", 0), ("outer", 0), ("outer", 1), ("msg", 0), ("msg", 1),
                    ("msgT", 0), ("merge", 0), ("scale", 1), ("catT", 0), ("up", 0), ("down", 0), ("scale", 2),
                    ("norm", 3), ("scale", 3), ("routeT", 0), ("route", 0), ("pick", 0)):
        yield kind, a
    for t in range(TS + 1):
        if t < TS:
            yield "hidden", t
        if t >= 1:
            yield "hiddenT", t - 1
    yield "pickT", 0
    yield "expert", 0
    for kind, n in (("norm", 1), ("scale", 1), ("attnT", 1), ("k4", 1), ("q4", 4), ("v4", 1)):
        for a in range(n):
            yield kind, 4 if kind in ("norm", "scale") else a
    for t in range(TS + 2):
        if t < TS:
            yield "score", t
        if 1 <= t <= TS:
            yield "soft", t - 1
        if t >= 2:
            yield "blend", t - 2
    for kind, n in (("attend", 1), ("norm", 1), ("scale", 1), ("ffnT", 1), ("ffn1", 2), ("gate", 1), ("gates", 1), ("gateT", 1),
                    ("ffn2", TS), ("ffnb", 1), ("result", 1)):
        for a in range(n):
            yield kind, 5 if kind in ("norm", "scale") else a


STAGES = tuple(stream_stages())


class Chunk:

    def __init__(self, register):
        self.register = register

    def count(self, per_chunk, n):
        return self.register * per_chunk + n


def in_turns(chunk):
    return [(s, chunk, kind, a) for kind, a in STAGES for s in range(STREAMS)]


def bank_uses(mine):
    return {st: n + 1 for n, st in enumerate(st for st in STAGES if st[0] not in NO_BANK and mine(st[0]))}


NORM_OF = {"merge": 1, "down": 2}
D_AFTER = bank_uses(lambda kind: kind not in ACT_TAKES)
A_AFTER = bank_uses(lambda kind: kind in ACT_TAKES)
D_USES, A_USES = len(D_AFTER), len(A_AFTER)
assert D_USES % D_BANKS == 0 and A_USES % A_BANKS == 0


def tokens(nc, ctx, d, tok, out):
    def sb(name, shape):
        return ctx.enter_context(nc.sbuf_tensor(name, shape, F32))

    def sem(name):
        return ctx.enter_context(nc.semaphore(name))

    def sems(name):
        return [sem(f"{name}{s}") for s in range(STREAMS)]

    w = {}
    loads = []
    for name in ("wq1", "wkv", "headmask", "wm", "w1", "w2", "g1", "b1", "g2", "b2", "rw", "ew1", "ew2", "eb2",
                 "rev32", "rev8", "wq4", "wk4", "wv4", "wo4", "fw1", "fwg", "bg", "fwd", "fbd"):
        w[name] = sb("t_" + name, list(d[name].shape))
        loads.append((w[name], d[name]))

    S2 = STREAMS
    ident = sb("t_ident", [128, 128])
    rows_in = sb("rows_in", [128, S2, TS, C])
    h = sb("h", [128, S2, TS, C])
    cat = sb("cat", [128, S2, TS, 2 * C])
    ext = sb("ext", [128, S2, TS, 128])
    xT = sb("xT", [128, S2, NT])
    centered, squared = sb("centered", [128, S2, TS, C]), sb("squared", [128, S2, TS, C])
    mean, var, std, rstd = (sb(n, [128, S2, TS]) for n in ("mean", "var", "std", "rstd"))
    eps = sb("eps", [128, 1])
    wide = sb("wide", [128, S2, TS, C])
    q_exp = sb("q_exp", [64, S2, NT])
    Q = sb("Q", [128, S2, NT])
    k_exp, K = (sb(n, [128, S2, TS, C]) for n in ("k_exp", "K"))
    V = sb("V", [128, S2, TS, 2, 128])
    KV = sb("KV", [128, S2, TS, 2, 128])
    den = sb("den", [128, S2, TS, HEADS])
    upT = sb("upT", [128, S2, NT])
    logits, hit = sb("logits", [128, S2, TS, EXPERTS]), sb("hit", [128, S2, TS, EXPERTS])
    pick = sb("pick", [128, S2, TS, EXPERTS])
    top, first = sb("top", [128, S2, TS]), sb("first", [128, S2, TS])
    pickT = sb("pickT", [128, S2, 128])
    hidden = sb("hidden", [128, S2, 2, EXPERTS * EHID])
    hiddenT = sb("hiddenT", [128, S2, TS, 4, 128])
    q4 = sb("q4", [128, S2, 4, NT])
    K4 = sb("K4", [128, S2, 2 * TS, 2, 64])
    V4 = sb("V4", [128, S2, 2 * TS, 64])
    attn = sb("attn", [128, S2, 3, HEADS, 64])
    total = sb("total", [128, S2, HEADS])
    peak, scale = (sb(n, [128, S2, 2, HEADS]) for n in ("peak", "scale"))
    blend = sb("blend", [128, S2, TS, 2, 64])
    fT = sb("fT", [128, S2, 2, NT])
    gl, ge, gp, gh, gw = (sb(n, [128, S2, TS, FEXPERTS]) for n in ("gl", "ge", "gp", "gh", "gw"))
    gtop, gsum, grec = (sb(n, [128, S2, TS]) for n in ("gtop", "gsum", "grec"))
    gwT = sb("gwT", [128, S2, 128])
    chosen = sb("chosen", [128, S2, 2, FEXPERTS, 64])
    ffn = sb("ffn", [128, S2, TS, C])
    result = sb("result", [128, S2, TS, C])
    d_banks = [[ctx.enter_context(nc.psum_tensor(f"d_bank{s}{i}", [128, 512], F32)) for i in range(D_BANKS)] for s in range(S2)]
    a_banks = [[ctx.enter_context(nc.psum_tensor(f"a_bank{s}{i}", [128, 512], F32)) for i in range(A_BANKS)] for s in range(S2)]

    weights_in, rows_read, stored = sem("weights_in"), sems("rows_read"), sems("stored")
    rows_used, result_free = sems("rows_used"), sems("result_free")
    t_ready, cleared = sem("t_ready"), sem("t_cleared")
    d_filled, d_emptied = sems("d_filled"), sems("d_emptied")
    a_filled, a_emptied = sems("a_filled"), sems("a_emptied")
    normed, picked, attn_ready, gate_ready = sems("normed"), sems("picked"), sems("attn_ready"), sems("gate_ready")
    gate_logits, result_ready = sems("gate_logits"), sems("result_ready")
    q_exped, k_exped, exped, gate_exped = sems("q_exped"), sems("k_exped"), sems("exped"), sems("gate_exped")
    store_begun = sem("store_begun")
    has_var, has_std = sems("has_var"), sems("has_std")
    dve_step, act_step = sem("dve_step"), sem("act_step")
    READY = 9

    block = ctx.enter_context(nc.Block())

    @block.sync
    def _(sp):
        tok_v = tok.rearrange("(q s t p) c -> q p s t c", q=QUARTERS, s=S2, p=128)
        for s in range(S2):
            sp.dma_start(rows_in[:, s, :, :], tok_v[0, :, s, :, :]).then_inc(rows_read[s], 16)
        for dst, src in loads:
            full = tuple(slice(None) for _ in dst.shape)
            sp.dma_start(dst[full], src).then_inc(weights_in, 16)
        with sp.Fori(0, QUARTERS - 1) as c:
            for s in range(S2):
                sp.wait_ge(rows_used[s], c + 1)
                sp.dma_start(rows_in[:, s, :, :], tok_v[bass.ds(c + 1, 1), :, s, :, :].rearrange("a p t c -> (a p) t c")) \
                  .then_inc(rows_read[s], 16)
            for s in range(S2):
                sp.wait_ge(stored[s], 16 * c + 16)
                sp.sem_inc(result_free[s], 1)
        for s in range(S2):
            sp.wait_ge(stored[s], 16 * QUARTERS)

    @block.gpsimd
    def _(pool):
        zeros = (ident[:, :], cat[:, :, :, :], ext[:, :, :, :], V[:, :, :, :, :])
        for zero in zeros:
            pool.memset(zero, 0.0).then_inc(t_ready, 1)
        pool.memset(eps[:, :], LN_EPS).then_inc(t_ready, 1)
        pool.wait_ge(t_ready, 5)
        pool.affine_select(out=ident[:, :], in_=ident[:, :], compare_op=ALU.not_equal, fill=1.0,
                           base=0, pattern=[[-1, 128]], channel_multiplier=1).then_inc(t_ready, 1)
        pool.wait_ge(t_ready, 6)
        pool.memset(ext[:, :, :, C:C + 1], 1.0).then_inc(t_ready, 1)
        for i in range(2):
            pool.wait_ge(t_ready, 7 + i)
            pool.memset(V[64 * i:64 * i + 64, :, :, i, 64:128], 1.0).then_inc(t_ready, 1)
        for s in range(S2):
            pool.sem_inc(d_emptied[s], D_BANKS)
            pool.sem_inc(a_emptied[s], A_BANKS)
            pool.sem_inc(result_free[s], 1)
        out_v = out.rearrange("(q s t p) c -> q p s t c", q=QUARTERS, s=S2, p=128)
        with pool.Fori(0, QUARTERS) as c:
            for s in range(S2):
                pool.wait_ge(result_ready[s], c + 1)
                pool.sem_inc(store_begun, 1)
                pool.dma_start(out_v[bass.ds(c, 1), :, s, :, :].rearrange("a p t c -> (a p) t c"), result[:, s, :, :]).then_inc(stored[s], 16)

    @block.tensor
    def _(pe):
        pe.wait_ge(weights_in, 16 * len(loads))
        pe.wait_ge(t_ready, READY)
        pe.wait_ge(cleared, 4)

        with pe.Fori(0, QUARTERS) as lap:
            for s, c, kind, a in in_turns(Chunk(lap)):
                if kind in NO_BANK:
                    continue
                for_act = kind in ACT_TAKES

                used = (A_AFTER if for_act else D_AFTER)[(kind, a)]
                bank = (a_banks[s][(used - 1) % A_BANKS]) if for_act else (d_banks[s][(used - 1) % D_BANKS])
                d_count, a_count = (0, used) if for_act else (used, 0)

                def copied(kind_before, a_before=0):
                    nonlocal d_count, a_count
                    key = (kind_before, a_before)
                    if kind_before in ACT_TAKES:
                        a_count = max(a_count, A_BANKS + A_AFTER[key])
                    else:
                        d_count = max(d_count, D_BANKS + D_AFTER[key])

                def by_tile(step, terms):
                    for t in range(TS):
                        pairs = terms(t)
                        for k, (lhs, rhs) in enumerate(pairs):
                            mm = pe.matmul(bank[:, step * t:step * t + WIDE], lhs, rhs, start=(k == 0), stop=(k == len(pairs) - 1))
                    return mm

                if kind in NORM_BEFORE:
                    pe.wait_ge(normed[s], c.count(NORMS, NORM_BEFORE[kind]))
                elif kind == "msgT":
                    copied("msg", TS // 2 - 1)
                elif kind in ("qT", "kv"):
                    copied("xT")
                elif kind == "outer" and a == 0:
                    copied("kv")
                elif kind == "msg":
                    copied("outer", a)
                elif kind == "merge":
                    copied("msgT")
                elif kind == "up":
                    copied("catT")
                elif kind == "down":
                    copied("up")
                elif kind in ("route", "hidden") and a == 0:
                    copied("routeT")
                elif kind == "hiddenT":
                    copied("hidden", a)
                elif kind == "pickT":
                    pe.wait_ge(picked[s], c.count(1, 1))
                elif kind == "expert":
                    copied("hiddenT", TS - 1)
                    copied("pickT")
                elif kind in ("q4", "k4", "v4") and a == 0:
                    copied("attnT")
                elif kind == "score" and a == 0:
                    copied("k4")
                    copied("q4", 3)
                elif kind == "blend":
                    pe.wait_ge(attn_ready[s], c.count(TS, a + 1))
                elif kind == "attend":
                    copied("blend", TS - 1)
                    copied("v4")
                elif kind == "ffn1" and a == 0:
                    copied("ffnT")
                elif kind == "gate":
                    copied("ffn1", 1)
                elif kind == "gateT":
                    pe.wait_ge(gate_ready[s], c.count(1, 1))
                elif kind == "ffnb":
                    copied("gateT")
                if d_count:
                    pe.wait_ge(d_emptied[s], c.count(D_USES, d_count))
                if a_count:
                    pe.wait_ge(a_emptied[s], c.count(A_USES, a_count))

                x = xT[:, s, :]
                if kind in ("xT", "msgT", "catT", "routeT", "attnT", "ffnT"):
                    src = cat if kind in ("xT", "msgT", "catT") else ext
                    for k in range(TS):
                        mm = pe.transpose(bank[:, 128 * k:128 * k + 128], src[:, s, k, :], ident[:, :])
                elif kind == "qT":
                    mm = pe.matmul(bank[0:64, :], w["wq1"][:, :], x, start=True, stop=True)
                elif kind == "kv":
                    for k in range(TS):
                        mm = pe.matmul(bank[:, 128 * k:128 * k + 128], xT[:, s, 128 * k:128 * k + 128], w["wkv"][:, :], start=True, stop=True)
                elif kind == "outer":
                    for k in range(2):
                        t = 2 * a + k
                        mm = pe.matmul(bank[0:64, 256 * k:256 * k + 256], K[:, s, t, :], V[:, s, t, :, :], start=True, stop=True)
                elif kind == "msg":
                    for k in range(2):
                        t = 2 * a + k
                        mm = pe.matmul(bank[:, 256 * k:256 * k + 256], Q[:, s, 128 * t:128 * t + 128], KV[:, s, t, :, :], start=True, stop=True)
                elif kind == "merge":
                    mm = by_tile(C, lambda t: [(xT[:, s, 128 * t:128 * t + 128], w["wm"][:, :])])
                elif kind == "up":
                    mm = pe.matmul(bank[:, :], w["w1"][:, :], x, start=True, stop=True)
                elif kind == "down":
                    mm = by_tile(C, lambda t: [(upT[:, s, 128 * t:128 * t + 128], w["w2"][:, :])])
                elif kind == "route":
                    mm = by_tile(EXPERTS, lambda t: [(xT[:, s, 128 * t:128 * t + 128], w["rw"][:, :])])
                elif kind == "hidden":
                    mm = pe.matmul(bank[:, :], xT[:, s, 128 * a:128 * a + 128], w["ew1"][:, :], start=True, stop=True)
                elif kind == "hiddenT":
                    for k in range(4):
                        mm = pe.transpose(bank[:, 128 * k:128 * k + 128], hidden[:, s, a % 2, 128 * k:128 * k + 128], ident[:, :])
                elif kind == "pickT":
                    mm = pe.transpose(bank[:, 0:128], pick[:, s, :, :], ident[:, :])
                elif kind == "expert":
                    mm = by_tile(C, lambda t: [(hiddenT[:, s, t, k, :], w["ew2"][:, k, :]) for k in range(4)]
                                 + [(pickT[:, s, :], w["eb2"][:, t, :])])
                elif kind == "q4":
                    mm = pe.matmul(bank[:, :], w["wq4"][:, a, :], x, start=True, stop=True)
                elif kind == "k4":
                    mm = pe.matmul(bank[:, :], w["wk4"][:, :], x, start=True, stop=True)
                elif kind == "v4":
                    mm = pe.matmul(bank[:, :], w["wv4"][:, :], x, start=True, stop=True)
                elif kind == "score":
                    for p in range(4):
                        for i in range(2):
                            img = 2 * a + i
                            mm = pe.matmul(bank[64 * i:64 * i + 64, 128 * p:128 * p + 128], q4[:, s, p, 64 * img:64 * img + 64],
                                           K4[:, s, img, :, :], start=True, stop=True)
                elif kind == "blend":
                    for p in range(4):
                        for odd in range(2):
                            mm = pe.matmul(bank[64 * odd:64 * odd + 64, 0:128], attn[:, s, a % 3, 2 * p + odd, :], w["wo4"][:, 2 * p + odd, :],
                                           start=(p == 0), stop=(p == 3))
                elif kind == "attend":
                    for t in range(TS):
                        for i in range(2):
                            mm = pe.matmul(bank[64 * i:64 * i + 64, 64 * t:64 * t + 64], V4[:, s, 2 * t + i, :], blend[:, s, t, i, :],
                                           start=True, stop=True)
                elif kind == "ffn1":
                    mm = pe.matmul(bank[:, :], w["fw1"][:, 128 * a:128 * a + 128], x, start=True, stop=True)
                elif kind == "gate":
                    mm = by_tile(FEXPERTS, lambda t: [(fT[:, s, k, 128 * t:128 * t + 128], w["fwg"][:, k, :]) for k in range(2)])
                elif kind == "gateT":
                    mm = pe.transpose(bank[0:TS * FEXPERTS, 0:128], gw[:, s, :, :], ident[:, :])
                elif kind == "ffn2":
                    for k in range(2):
                        mm = pe.matmul(bank[:, :], fT[:, s, k, 128 * a:128 * a + 128], w["fwd"][:, k, :], start=(k == 0), stop=(k == 1))
                elif kind == "ffnb":
                    mm = by_tile(C, lambda t: [(gwT[:, s, :], w["fbd"][:, t, :])])
                mm.then_inc(a_filled[s] if for_act else d_filled[s], 1)

    @block.scalar
    def _(act):
        act.wait_ge(t_ready, READY)
        steps = [0]

        with act.Fori(0, QUARTERS) as lap:
            for s, c, kind, a in in_turns(Chunk(lap)):
                def filled():
                    act.wait_ge(d_filled[s], c.count(D_USES, D_AFTER[(kind, a)]))
                    return d_banks[s][(D_AFTER[(kind, a)] - 1) % D_BANKS]

                def exp_below_zero(dst, src, done):
                    act.activation(dst, src, ACT.Relu, scale=-1.0).then_inc(act_step, 1)
                    steps[0] += 1
                    act.wait_ge(act_step, lap * (2 * STREAMS) + steps[0])
                    act.activation(dst, dst, ACT.Exp, scale=-1.0).then_inc(done, 1)

                if kind in ("norm", "merge", "down"):
                    act.wait_ge(has_var[s], c.count(NORMS, NORM_OF.get(kind, a) + 1))
                    act.activation(std[:, s, :], var[:, s, :], ACT.Sqrt, bias=eps[:, 0:1], scale=1.0 / C).then_inc(has_std[s], 1)
                elif kind == "qT":
                    exp_below_zero(q_exp[:, s, :], filled()[0:64, :], q_exped[s])
                elif kind == "kv":
                    b = filled()[:, :].rearrange("p (t k) -> p t k", t=TS)
                    exp_below_zero(k_exp[:, s, :, :], b[:, :, 0:64], k_exped[s])
                elif kind == "score":
                    act.wait_ge(d_emptied[s], c.count(D_USES, D_BANKS + D_AFTER[(kind, a)]))
                    slot = attn[:, s, a % 3, :, :]
                    act.activation(slot, slot, ACT.Exp, scale=8.0 ** -0.5).then_inc(exped[s], 1)
                elif kind == "gates":
                    act.wait_ge(gate_logits[s], c.count(1, 1))
                    act.activation(ge[:, s, :, :], ge[:, s, :, :], ACT.Exp).then_inc(gate_exped[s], 1)
                elif kind in ACT_TAKES:
                    used = A_AFTER[(kind, a)]
                    act.wait_ge(a_filled[s], c.count(A_USES, used))
                    b = a_banks[s][(used - 1) % A_BANKS]
                    fn = ACT.Copy
                    if kind in ("xT", "msgT", "catT", "routeT", "attnT", "ffnT"):
                        dst = xT[:, s, :]
                    elif kind == "up":
                        dst, fn = upT[:, s, :], ACT.Relu
                    elif kind == "hiddenT":
                        dst = hiddenT[:, s, a, :, :].rearrange("p k n -> p (k n)")
                    elif kind == "q4":
                        dst = q4[:, s, a, :]
                    elif kind == "v4":
                        dst = V4[:, s, :, :].rearrange("p i k -> p (i k)")
                    else:
                        dst, fn = fT[:, s, a, :], ACT.Gelu
                    act.activation(dst, b[:, :], fn).then_inc(a_emptied[s], 1)

    @block.vector
    def _(dve):
        for zero in (Q[:, :, :], KV[:, :, :, :, :], K4[:, :, :, :, :], gwT[:, :, :]):
            dve.memset(zero, 0.0).then_inc(cleared, 1)
        dve.wait_ge(cleared, 4)
        dve.wait_ge(weights_in, 16 * len(loads))
        dve.wait_ge(t_ready, READY)
        DVE_STEPS = 60
        steps = [0]

        with dve.Fori(0, QUARTERS) as lap:
            def link(ins):
                ins.then_inc(dve_step, 1)
                steps[0] += 1
                dve.wait_ge(dve_step, lap * (DVE_STEPS * STREAMS) + steps[0])

            def taken():
                dve.wait_ge(d_emptied[s], c.count(D_USES, D_BANKS + D_AFTER[(kind, a)]))

            def wide_of(ap, n):
                return ap.unsqueeze(2).to_broadcast([128, ap.shape[1], n])

            def centre(src):
                link(dve.tensor_reduce(mean[:, s, :], src, AX.X, ALU.add))
                return dve.scalar_tensor_tensor(out=centered[:, s, :, :], in0=wide_of(mean[:, s, :], C), scalar=-1.0 / C, in1=src,
                                                op0=ALU.mult, op1=ALU.add)

            def spread():
                x = centered[:, s, :, :]
                link(dve.tensor_tensor(squared[:, s, :, :], x, x, ALU.mult))
                dve.tensor_reduce(var[:, s, :], squared[:, s, :, :], AX.X, ALU.add).then_inc(has_var[s], 1)

            for s, c, kind, a in in_turns(Chunk(lap)):
                if kind not in NO_BANK and kind not in ACT_TAKES:
                    used = D_AFTER[(kind, a)]
                    dve.wait_ge(d_filled[s], c.count(D_USES, used))
                    bank = d_banks[s][(used - 1) % D_BANKS]
                    by_tile = bank[:, 0:TS * C].rearrange("p (t k) -> p t k", t=TS)

                if kind == "norm":
                    if a == 0:
                        dve.wait_ge(rows_read[s], c.count(16, 16))
                    link(centre(rows_in[:, s, :, :] if a == 0 else h[:, s, :, :]))
                    spread()
                elif kind == "scale":
                    x, rows = centered[:, s, :, :], [128, TS, C]
                    dve.wait_ge(has_std[s], c.count(NORMS, a + 1))
                    link(dve.reciprocal(rstd[:, s, :], std[:, s, :]))
                    gain = {1: (w["g1"], w["b1"], cat[:, s, :, C:2 * C]), 2: (w["g2"], w["b2"], wide[:, s, :, :])}.get(a)
                    if gain is None:
                        dst = cat[:, s, :, 0:C] if a == 0 else ext[:, s, :, 0:C]
                        dve.tensor_tensor(dst, x, wide_of(rstd[:, s, :], C), ALU.mult).then_inc(normed[s], 1)
                        continue
                    link(dve.tensor_tensor(x, x, wide_of(rstd[:, s, :], C), ALU.mult))
                    link(dve.tensor_tensor(x, x, gain[0][:, :].unsqueeze(1).to_broadcast(rows), ALU.mult))
                    dve.tensor_tensor(gain[2], x, gain[1][:, :].unsqueeze(1).to_broadcast(rows), ALU.add).then_inc(normed[s], 1)
                    if a == 2:
                        dve.wait_ge(normed[s], c.count(NORMS, 3))
                        link(dve.tensor_tensor(wide[:, s, :, :], wide[:, s, :, :], cat[:, s, :, 0:C], ALU.add))
                        dve.tensor_tensor(h[:, s, :, :], rows_in[:, s, :, :], wide[:, s, :, :], ALU.add).then_inc(rows_used[s], 1)
                        dve.wait_ge(rows_used[s], c.count(1, 1))

                elif kind == "qT":
                    dve.wait_ge(q_exped[s], c.count(1, 1))
                    dve.scalar_tensor_tensor(out=Q[0:64, s, :], in0=bank[0:64, :], scalar=0.0, in1=q_exp[:, s, :], op0=ALU.max,
                                             op1=ALU.add).then_inc(d_emptied[s], 1)
                elif kind == "kv":
                    b = bank[:, :].rearrange("p (t k) -> p t k", t=TS)
                    dve.wait_ge(k_exped[s], c.count(1, 1))
                    for i in range(2):
                        rows = slice(64 * i, 64 * i + 64)
                        dve.tensor_copy(V[rows, s, :, i, 0:64], b[rows, :, 64:128])
                    dve.scalar_tensor_tensor(out=K[:, s, :, :], in0=b[:, :, 0:64], scalar=0.0, in1=k_exp[:, s, :, :], op0=ALU.max,
                                             op1=ALU.add).then_inc(d_emptied[s], 1)
                elif kind == "outer":
                    b = bank[0:64, :].rearrange("p (n k) -> p n k", n=4)
                    dst = KV[0:64, s, 2 * a:2 * a + 2, :, :].rearrange("p t i k -> p (t i) k")
                    dve.tensor_tensor(dst, b, w["headmask"][:, :].unsqueeze(1).to_broadcast([64, 4, 128]), ALU.mult).then_inc(d_emptied[s], 1)
                elif kind == "msg":
                    b = bank[:, :].rearrange("p (t i k) -> p t i k", t=2, i=2)
                    two = slice(2 * a, 2 * a + 2)
                    dve.tensor_scalar(den[0:64, s, two, :], b[0:64, :, 0, 64:128:8], ATT_EPS, None, ALU.add)
                    link(dve.tensor_scalar(den[64:128, s, two, :], b[64:128, :, 1, 64:128:8], ATT_EPS, None, ALU.add))
                    link(dve.reciprocal(den[:, s, two, :], den[:, s, two, :]))
                    for i in range(2):
                        rows = slice(64 * i, 64 * i + 64)
                        last = dve.tensor_tensor(cat[rows, s, two, C:2 * C].rearrange("p t (h v) -> p t h v", h=HEADS),
                                                 b[rows, :, i, 0:64].rearrange("p t (h v) -> p t h v", h=HEADS),
                                                 den[rows, s, two, :].unsqueeze(3).to_broadcast([64, 2, HEADS, C // HEADS]), ALU.mult)
                    last.then_inc(d_emptied[s], 1)
                elif kind == "merge":
                    centre(by_tile).then_inc(d_emptied[s], 1)
                    taken()
                    spread()
                elif kind == "down":
                    centre(by_tile).then_inc(d_emptied[s], 1)
                    taken()
                    spread()

                elif kind == "route":
                    dve.tensor_copy(logits[:, s, :, :], bank[:, 0:TS * EXPERTS].rearrange("p (t e) -> p t e", t=TS)).then_inc(d_emptied[s], 1)
                    taken()
                elif kind == "pick":
                    rows = [128, TS, EXPERTS]
                    link(dve.tensor_reduce(top[:, s, :], logits[:, s, :, :], AX.X, ALU.max))
                    link(dve.tensor_tensor(hit[:, s, :, :], logits[:, s, :, :], wide_of(top[:, s, :], EXPERTS), ALU.is_equal))
                    link(dve.tensor_tensor(hit[:, s, :, :], hit[:, s, :, :], w["rev32"][:, :].unsqueeze(1).to_broadcast(rows), ALU.mult))
                    link(dve.tensor_reduce(first[:, s, :], hit[:, s, :, :], AX.X, ALU.max))
                    dve.tensor_tensor(pick[:, s, :, :], hit[:, s, :, :], wide_of(first[:, s, :], EXPERTS), ALU.is_equal).then_inc(picked[s], 1)
                    dve.wait_ge(picked[s], c.count(1, 1))
                elif kind == "hidden":
                    dst = hidden[:, s, a % 2, :].rearrange("p (e k) -> p e k", e=EXPERTS)
                    dve.scalar_tensor_tensor(out=dst, in0=bank[:, :].rearrange("p (e k) -> p e k", e=EXPERTS), scalar=0.0,
                                             in1=wide_of(pick[:, s, a, :], EHID), op0=ALU.max, op1=ALU.mult).then_inc(d_emptied[s], 1)
                elif kind == "pickT":
                    dve.tensor_copy(pickT[:, s, :], bank[:, 0:128]).then_inc(d_emptied[s], 1)
                elif kind == "expert":
                    dve.scalar_tensor_tensor(out=h[:, s, :, :], in0=by_tile, scalar=0.0, in1=h[:, s, :, :],
                                             op0=ALU.max, op1=ALU.add).then_inc(d_emptied[s], 1)
                    taken()

                elif kind == "k4":
                    b = bank[:, :].rearrange("p (i t) -> p i t", t=64)
                    dve.tensor_copy(K4[0:64, s, :, 0, :], b[0:64, :, :])
                    dve.tensor_copy(K4[64:128, s, :, 1, :], b[64:128, :, :]).then_inc(d_emptied[s], 1)
                elif kind == "score":
                    b = bank[:, :].rearrange("p (h t) -> p h t", h=HEADS)
                    link(dve.tensor_reduce(peak[:, s, a % 2, :], b, AX.X, ALU.max))
                    dve.tensor_tensor(attn[:, s, a % 3, :, :], b, wide_of(peak[:, s, a % 2, :], 64), ALU.subtract).then_inc(d_emptied[s], 1)
                elif kind == "soft":
                    dve.wait_ge(exped[s], c.count(TS, a + 1))
                    slot = attn[:, s, a % 3, :, :]
                    link(dve.tensor_reduce(total[:, s, :], slot, AX.X, ALU.add))
                    link(dve.reciprocal(scale[:, s, a % 2, :], total[:, s, :]))
                    dve.tensor_tensor(slot, slot, wide_of(scale[:, s, a % 2, :], 64), ALU.mult).then_inc(attn_ready[s], 1)
                elif kind == "blend":
                    dve.tensor_copy(blend[:, s, a, :, :], bank[:, 0:128].rearrange("p (i k) -> p i k", i=2)).then_inc(d_emptied[s], 1)
                elif kind == "attend":
                    dve.tensor_tensor(h[:, s, :, :], by_tile, h[:, s, :, :], ALU.add).then_inc(d_emptied[s], 1)
                    taken()

                elif kind == "gate":
                    rows = [128, TS, FEXPERTS]
                    dve.tensor_tensor(gl[:, s, :, :], bank[:, 0:TS * FEXPERTS].rearrange("p (t e) -> p t e", t=TS),
                                      w["bg"][:, :].unsqueeze(1).to_broadcast(rows), ALU.add).then_inc(d_emptied[s], 1)
                    taken()
                    link(dve.tensor_reduce(gtop[:, s, :], gl[:, s, :, :], AX.X, ALU.max))
                    dve.tensor_tensor(ge[:, s, :, :], gl[:, s, :, :], wide_of(gtop[:, s, :], FEXPERTS), ALU.subtract).then_inc(gate_logits[s], 1)
                elif kind == "gates":
                    rows = [128, TS, FEXPERTS]
                    e, p, hits = ge[:, s, :, :], gp[:, s, :, :], gh[:, s, :, :]
                    dve.wait_ge(gate_exped[s], c.count(1, 1))
                    link(dve.tensor_reduce(gsum[:, s, :], e, AX.X, ALU.add))
                    link(dve.reciprocal(grec[:, s, :], gsum[:, s, :]))
                    link(dve.tensor_tensor(p, e, wide_of(grec[:, s, :], FEXPERTS), ALU.mult))
                    link(dve.tensor_reduce(gtop[:, s, :], p, AX.X, ALU.max))
                    link(dve.tensor_tensor(hits, p, wide_of(gtop[:, s, :], FEXPERTS), ALU.is_equal))
                    link(dve.tensor_tensor(hits, hits, w["rev8"][:, :].unsqueeze(1).to_broadcast(rows), ALU.mult))
                    link(dve.tensor_reduce(gsum[:, s, :], hits, AX.X, ALU.max))
                    link(dve.tensor_tensor(hits, hits, wide_of(gsum[:, s, :], FEXPERTS), ALU.is_equal))
                    dve.tensor_tensor(gw[:, s, :, :], hits, p, ALU.mult).then_inc(gate_ready[s], 1)
                    dve.wait_ge(gate_ready[s], c.count(1, 1))
                elif kind == "gateT":
                    dve.tensor_copy(gwT[0:TS * FEXPERTS, s, :], bank[0:TS * FEXPERTS, 0:128]).then_inc(d_emptied[s], 1)
                elif kind == "ffn2":
                    dst = chosen[:, s, a % 2, :, :]
                    dve.tensor_tensor(dst, bank[:, :].rearrange("p (e k) -> p e k", e=FEXPERTS), wide_of(gw[:, s, a, :], 64), ALU.mult) \
                       .then_inc(d_emptied[s], 1)
                    taken()
                    link(dve.tensor_reduce(ffn[:, s, a, :], dst.rearrange("p e k -> p k e"), AX.X, ALU.add))
                elif kind == "ffnb":
                    dve.tensor_tensor(wide[:, s, :, :], by_tile, h[:, s, :, :], ALU.add).then_inc(d_emptied[s], 1)
                    taken()
                elif kind == "result":
                    dve.wait_ge(result_free[s], c.count(1, 1))
                    dve.tensor_tensor(result[:, s, :, :], wide[:, s, :, :], ffn[:, s, :, :], ALU.add).then_inc(result_ready[s], 1)
        assert steps[0] == STREAMS * DVE_STEPS, steps[0]


def program(nc, d, out):
    with ExitStack() as ctx:
        tok = nc.dram_tensor("tok", (IMAGES, PIX), F32, kind="Internal").ap()
        tower(nc, ctx, d, tok)
    with ExitStack() as ctx:
        tokens(nc, ctx, d, tok.rearrange("b (s c) -> (b s) c", c=C), out.rearrange("b s c -> (b s) c"))


_OUTS = [((64, 64, 64), 'float32')]


def block_diagonal(a, n):
    out = np.zeros((n, a.shape[0], n, a.shape[1]), a.dtype)
    for i in range(n):
        out[i, :, i, :] = a
    return out.reshape(n * a.shape[0], n * a.shape[1])


def lay_out(x):
    f = np.float32
    one = np.ones((IMAGES, HEIGHT, WIDTH, 1), f)
    xa = np.concatenate([x["x"], one], axis=-1).reshape(QUARTERS, GROUPS, 4, 2, 32, WIDTH, J)
    fc0 = np.concatenate([x["L0_tok_fc0_w"], x["L0_tok_fc0_b"][None]], axis=0)
    sw = np.stack([x[f"L0_tok_sw{i}"] for i in range(LAYERS)])
    conv = [block_diagonal(x[f"L0_tok_cw{i}"].T, 4) for i in range(LAYERS)]
    fc1 = np.zeros((128, 2, 128), f)
    fc2 = np.zeros((128, 2, 32), f)
    for pair in range(2):
        fc1[64 * pair:64 * pair + 64, pair] = block_diagonal(x["L0_tok_fc1_w"], 2)
        fc2[:, pair, 2 * pair:2 * pair + 2] = block_diagonal(x["L0_tok_fc2_w"], 2)
    out = {
        "x_planes": xa.transpose(0, 1, 2, 6, 4, 3, 5).reshape(QUARTERS, GROUPS, 16, PIX),
        "x_pix": xa.transpose(0, 3, 5, 1, 6, 4, 2).reshape(QUARTERS, 128, GROUPS * J * 128),
        "spec_w": sw.reshape(LAYERS, CH, CH, KXM, 2, KYQ, 4).transpose(0, 6, 1, 5, 4, 3, 2).reshape(LAYERS, 128, -1),
        "conv_w": np.stack(conv, axis=1),
        "conv_b": np.stack([np.tile(x[f"L0_tok_cb{i}"], 4) for i in range(LAYERS)], axis=1),
        "lift_w": block_diagonal(block_diagonal(fc0, 4), KYQ), "lift_t": block_diagonal(fc0.T, 4),
        "fc1_w": fc1, "fc1_b": np.tile(x["L0_tok_fc1_b"], 2)[:, None],
        "fc2_w": fc2, "fc2_b": np.full((128, 1), x["L0_tok_fc2_b"][0]),
    }
    out.update(fourier_tables())

    def below(a, columns=0, rows=128, at=0):
        b = np.zeros((rows,) + a.shape[1:-1] + (max(columns, a.shape[-1]),), f)
        b[at:at + a.shape[0], ..., :a.shape[-1]] = a
        return b

    def with_bias(w, b):
        return np.concatenate([w, b[None]], axis=0)

    heads = np.arange(64) // 8
    rep = lambda v: np.tile(v[None], (128, 1))
    wq4 = x["L1_attn_Wq"].reshape(4, 128, 64).transpose(2, 0, 1)
    wo = x["L1_attn_Wo"].reshape(64, 64, 8).transpose(1, 2, 0)
    wo4 = np.zeros((2, 64, 8, 2, 64), f)
    wo4[0, :, :, 0], wo4[1, :, :, 1] = wo, wo
    eb2 = np.zeros((4, 32, 4, WIDE), f)
    fbd = np.zeros((16, 8, 8, WIDE), f)
    for t in range(4):
        eb2[t, :, t, :64] = x["L0_ffn_b2"]
    for t in range(8):
        fbd[t, :, t, :64] = x["L1_ffn_bd"]
    wk, wv = x["L1_attn_Wk"].T, x["L1_attn_Wv"].T
    out.update({
        "wq1": below(x["L0_attn_Wq"]), "wkv": below(np.concatenate([x["L0_attn_Wk"], x["L0_attn_Wv"]], axis=1)),
        "headmask": np.tile((heads[:, None] == heads[None, :]).astype(f), (1, 2)),
        "wm": below(x["L0_attn_Wm"], WIDE, at=64), "w1": x["L0_attn_W1"], "w2": below(x["L0_attn_W2"], WIDE),
        "g1": rep(x["L0_attn_g1"]), "b1": rep(x["L0_attn_b1"]), "g2": rep(x["L0_attn_g2"]), "b2": rep(x["L0_attn_b2"]),
        "rw": below(with_bias(x["L0_ffn_router_w"].T, x["L0_ffn_router_b"]), WIDE),
        "ew1": below(with_bias(x["L0_ffn_W1"].transpose(1, 0, 2).reshape(64, 512), x["L0_ffn_b1"].reshape(512))),
        "ew2": below(x["L0_ffn_W2"].reshape(4, 128, 64).transpose(1, 0, 2), WIDE), "eb2": eb2.reshape(128, 4, WIDE),
        "rev32": rep(np.arange(32, 0, -1).astype(f)), "rev8": rep(np.arange(8, 0, -1).astype(f)),
        "wq4": below(wq4), "wk4": below(np.concatenate([wk, wk], axis=1)), "wv4": below(np.concatenate([wv, wv], axis=1)),
        "wo4": wo4.reshape(128, 8, 128),
        "fw1": below(with_bias(x["L1_ffn_W1"], x["L1_ffn_b1"])),
        "fwg": below(x["L1_ffn_Wg"].reshape(2, 128, 8).transpose(1, 0, 2), WIDE), "bg": rep(x["L1_ffn_bg"]),
        "fwd": x["L1_ffn_Wd"].transpose(1, 0, 2).reshape(2, 128, 512).transpose(1, 0, 2), "fbd": fbd.reshape(128, 8, WIDE),
    })
    return {k: np.ascontiguousarray(v) for k, v in out.items()}


def kernel(**inputs):
    import concourse.bacc as _bacc
    from concourse.bass_utils import run_bass_kernel_spmd as _run

    nc = _bacc.Bacc("TRN2", target_bir_lowering=False, num_devices=1)
    laid = lay_out({k: np.asarray(v) for k, v in inputs.items()})
    d = {k: nc.dram_tensor(f"in_{k}", v.shape, mybir.dt.from_np(v.dtype), kind="ExternalInput").ap() for k, v in laid.items()}
    out = nc.dram_tensor("out_0", (64, 64, 64), F32, kind="ExternalOutput").ap()
    program(nc, d, out)
    r = _run(nc, [{f"in_{k}": v for k, v in laid.items()}], core_ids=[0])
    return r.results[0]["out_0"]
```
